# Optimizing a Trainium2 kernel written in Bass

```python
import numpy as np
import jax
import jax.numpy as jnp

def _softmax(x, axis=-1):
    return jax.nn.softmax(x, axis=axis)

def _gelu(x):
    return jax.nn.gelu(x, approximate=True)

def _silu(x):
    return jax.nn.silu(x)

def _sigmoid(x):
    return jax.nn.sigmoid(x)

def _layernorm(x, axis=-1, eps=1e-05):
    m = jnp.mean(x, axis=axis, keepdims=True)
    v = jnp.var(x, axis=axis, keepdims=True)
    return (x - m) / jnp.sqrt(v + eps)

def _scatter_add(tgt, idx, src, axis=0):
    return tgt.at[idx].add(src)

def _segment_sum(src, seg, n):
    return jax.ops.segment_sum(src, seg, n)
kernel_name = 'mk_adj_resnorm_d2_adj_r2_b4ab22'

def setup_inputs(seed: int=0):
    np.random.seed(seed)
    _w = jnp.asarray

    def _rec_inputs():
        import jax
        import jax.numpy as jnp
        _gk = jax.random.key(seed)
        x = -0.0002928 + 1 * jax.random.normal(jax.random.fold_in(_gk, 1), (8, 1024, 128), jnp.float32)
        _w = (1.0 + jnp.arange(1024, dtype=jnp.float32)) ** (-0.5)
        _w = _w / _w.mean()
        _pij = jnp.clip(0.00390625 * _w[:, None] * _w[None, :], 0.0, 1.0)
        _a = jax.random.uniform(jax.random.fold_in(_gk, 2), (1024, 1024)) < _pij
        adj = _a.astype(jnp.int32)
        return (x, adj)
    x, adj = _rec_inputs()

    def _L0_gnn_setup():
        import jax, jax.numpy as jnp
        import numpy as np
        NEG_BIG = -9000000000000000.0
        key = jax.random.key(seed)
        k1, k2, k3, k4 = jax.random.split(key, 4)
        bs, N, Fin, Fout = (8, 1024, 128, 128)
        x = jax.random.normal(k1, (bs, N, Fin), dtype=jnp.float32)
        adj = jax.random.randint(k2, (N, N), 0, 2, dtype=jnp.int32)
        W = jax.random.normal(k3, (Fin, Fout), dtype=jnp.float32) * (1.414 / np.sqrt(Fin))
        a = jax.random.normal(k4, (2 * Fout, 1), dtype=jnp.float32) * 0.1
        return {'x': x, 'adj': adj, 'W': W, 'a': a}
    _L0_gnn_all = _L0_gnn_setup()
    _L0_gnn_in = {k: v for k, v in _L0_gnn_all.items() if k in ('W', 'a')}
    del _L0_gnn_all

    def _L1_gnn_setup():
        import jax, jax.numpy as jnp
        import numpy as np
        ALPHA = 0.2
        EPS = 1e-06
        key = jax.random.key(seed)
        ks = jax.random.split(key, 8)
        B, N, D, H = (2, 1024, 128, 8)
        dh = D // H
        x = jax.random.normal(ks[0], (B, N, D), dtype=jnp.float32)
        adj = jax.random.randint(ks[1], (N, N), 0, 2, dtype=jnp.int32)
        adj = jnp.maximum(adj, jnp.eye(N, dtype=jnp.int32))
        p = jax.random.uniform(ks[2], (B, N, N), dtype=jnp.float32)
        prior = p / jnp.sum(p, axis=-1, keepdims=True)
        W = jax.random.normal(ks[3], (H, D, dh), dtype=jnp.float32) * (1.0 / np.sqrt(D))
        a_src = jax.random.normal(ks[4], (H, dh), dtype=jnp.float32) * (1.0 / np.sqrt(dh))
        a_dst = jax.random.normal(ks[5], (H, dh), dtype=jnp.float32) * (1.0 / np.sqrt(dh))
        beta_tilde = jnp.ones((), dtype=jnp.float32)
        W_out = jax.random.normal(ks[6], (D, D), dtype=jnp.float32) * (1.0 / np.sqrt(D))
        return {'x': x, 'adj': adj, 'prior': prior, 'W': W, 'a_src': a_src, 'a_dst': a_dst, 'beta_tilde': beta_tilde, 'W_out': W_out}
    _L1_gnn_all = _L1_gnn_setup()
    _L1_gnn_in = {k: v for k, v in _L1_gnn_all.items() if k in ('W', 'a_src', 'a_dst', 'beta_tilde', 'W_out')}
    del _L1_gnn_all
    return {'x': x, 'adj': adj, 'L0_gnn_W': _L0_gnn_in['W'], 'L0_gnn_a': _L0_gnn_in['a'], 'L1_gnn_W': _L1_gnn_in['W'], 'L1_gnn_a_src': _L1_gnn_in['a_src'], 'L1_gnn_a_dst': _L1_gnn_in['a_dst'], 'L1_gnn_beta_tilde': _L1_gnn_in['beta_tilde'], 'L1_gnn_W_out': _L1_gnn_in['W_out']}

def reference(x, adj, L0_gnn_W, L0_gnn_a, L1_gnn_W, L1_gnn_a_src, L1_gnn_a_dst, L1_gnn_beta_tilde, L1_gnn_W_out):
    import jax
    import jax.numpy as jnp

    def _L0_gnn_ref(x, adj, W, a):
        import jax, jax.numpy as jnp
        import numpy as np
        NEG_BIG = -9000000000000000.0
        alpha = 0.2
        h = jnp.matmul(x, W)
        Fout = h.shape[-1]
        a1, a2 = (a[:Fout, 0], a[Fout:, 0])
        s1 = jnp.einsum('bnf,f->bn', h, a1)
        s2 = jnp.einsum('bnf,f->bn', h, a2)
        e = jax.nn.leaky_relu(s1[:, :, None] + s2[:, None, :], negative_slope=alpha)
        attention = jnp.where(adj[None, :, :] > 0, e, NEG_BIG)
        attention = jax.nn.softmax(attention, axis=-1)
        h_prime = jnp.matmul(attention, h)
        return jax.nn.elu(h_prime)

    def _L1_gnn_ref(x, adj, prior, W, a_src, a_dst, beta_tilde, W_out):
        import jax, jax.numpy as jnp
        import numpy as np
        ALPHA = 0.2
        EPS = 1e-06
        B, N, D = x.shape
        x_proj = jnp.einsum('bnd,hdf->bhnf', x, W)
        e_src = jnp.einsum('bhnf,hf->bhn', x_proj, a_src)
        e_dst = jnp.einsum('bhnf,hf->bhn', x_proj, a_dst)
        e = jax.nn.leaky_relu(e_src[..., :, None] + e_dst[..., None, :], ALPHA)
        beta = jax.nn.softplus(beta_tilde)
        e = e + (beta * jnp.log(prior + EPS))[:, None, :, :]
        neg_inf = jnp.finfo(e.dtype).min
        e = jnp.where(adj[None, None, :, :] > 0, e, neg_inf)
        attn = jax.nn.softmax(e, axis=-1)
        h = jnp.einsum('bhij,bhjf->bhif', attn, x_proj)
        h = h.transpose(0, 2, 1, 3).reshape(B, N, D)
        return h @ W_out.T
    x = _layernorm(x + _L0_gnn_ref(x, adj, L0_gnn_W, L0_gnn_a), axis=-1)
    x = _layernorm(x + _L1_gnn_ref(x, adj, adj[None], L1_gnn_W, L1_gnn_a_src, L1_gnn_a_dst, L1_gnn_beta_tilde, L1_gnn_W_out), axis=-1)
    return x

_drawn_inputs = setup_inputs


def setup_inputs(seed=0):
    import zlib

    import numpy as np

    out = dict(_drawn_inputs(seed))
    spreads = {}
    factors = {}
    for name, (base, spread) in spreads.items():
        noise = np.random.default_rng([zlib.crc32(name.encode()), seed]).standard_normal(out[name].shape)
        drawn = base * np.exp(spread * noise) if base else spread * noise
        out[name] = jnp.asarray(drawn.astype(out[name].dtype))
    for name, factor in factors.items():
        out[name] = (out[name] * factor).astype(out[name].dtype)
    return out
```

```python
import concourse.bass as bass
from concourse import mybir
from contextlib import ExitStack

F32 = mybir.dt.float32
BF16 = mybir.dt.bfloat16
U8 = mybir.dt.uint8
FP8 = mybir.dt.float8e4
I32 = mybir.dt.int32
ALU = mybir.AluOpType
ACT = mybir.ActivationFunctionType
AX = mybir.AxisListType
RMAX = bass.bass_isa.ReduceOp.max

P = 128
BS, N, D, H = 8, 1024, 128, 8
NT = N // P
DH = D // H
NH = BS * H
KW = DH + 1
VW = 2 * KW
SLOPE = 0.2
LN_EPS = 1e-5
LOG_EPS = 1e-6
STEEP = 2.0 ** 60
EDGE_SHIFT = 5
EDGE_BYTE = 1 << EDGE_SHIFT
EDGE = 0.125
AC = 5


class Links:

    def __init__(self, eng, sem, per):
        self.eng, self.sem, self.per = eng, sem, per

    def begin(self, b):
        self.b, self.k = b, 0

    def link(self, ins):
        self.k += 1
        ins.then_inc(self.sem, 1)
        self.eng.wait_ge(self.sem, self.b * self.per + self.k)

    def end(self):
        assert self.k == self.per, (self.k, self.per)


def gnn_kernel(nc, x, adj, w0, a0, w1, a_src, a_dst, beta, w_out, out):
    ctx = ExitStack()
    with ctx:
        def sb(name, shape, dt=F32, where=ctx):
            return where.enter_context(nc.sbuf_tensor(name, shape, dt))

        def sem(name):
            return ctx.enter_context(nc.semaphore(name))

        x1_dram = nc.dram_tensor("x1_scratch", (BS, N, D), F32, kind="Internal").ap()
        es_dram = nc.dram_tensor("es_scratch", (NH, N), F32, kind="Internal").ap()

        ident = sb("ident", [P, P])
        identb = sb("identb", [P, P], BF16)
        ones_col = sb("ones_col", [P, 1], BF16)
        Gt = sb("Gt", [P, NT, N], FP8)
        GtN = sb("GtN", [P, NT, N], FP8)
        emptyf = sb("emptyf", [P, N])
        emptyb = sb("emptyb", [P, N], BF16)
        W0 = sb("W0", [P, D + 1])
        Wa1 = sb("Wa1", [P, P])
        W1 = sb("W1", [P, D + 2 * H])
        WoT = sb("WoT", [P, D])
        xp = sb("xp", [P, NT, BS * D])
        edes = sb("edes", [P, NT, 2, NH])
        csum1 = sb("csum1", [1, BS * D])
        lp = sb("lp", [P, 1])
        tiny = sb("tiny", [P, 8])
        stats = sb("stats", [P, NT, 6])
        mv = sb("mv", [P, NT, 2])
        rstd = sb("rstd", [P, NT])
        rstd_e = sb("rstd_e", [P, NT])
        lneps = sb("lneps", [P, NT])
        mhalf = sb("mhalf", [P, NT])
        rden = sb("rden", [P, NT * H])
        rslope = sb("rslope", [P, 1])
        idle = sb("idle", [P, 1])
        idle_v = sb("idle_v", [P, 1])

        L0 = ExitStack()
        xin = [sb(f"xin{q}", [P, NT, D], F32, L0) for q in range(2)]
        xres0 = [sb(f"xres0{q}", [P, NT, D], F32, L0) for q in range(2)]
        x1b = sb("x1b", [P, NT, D], F32, L0)
        xT = sb("xT", [P, N], F32, L0)
        x1T = sb("x1T", [P, N], F32, L0)
        hA = [sb(f"hA{q}", [P, NT, D + 1], F32, L0) for q in range(2)]
        Pt = [sb(f"Pt{q}", [P, NT, N], F32, L0) for q in range(2)]
        Rb = sb("Rb", [P, N], F32, L0)
        hp = sb("hp", [P, NT, D], F32, L0)
        et = sb("et", [P, NT, D], F32, L0)
        es_row = sb("es_row", [H, N], F32, L0)
        crow0 = [sb(f"crow0{q}", [P, D + 1], F32, L0) for q in range(2)]
        csx = [sb(f"csx_{q}", [P, 1], F32, L0) for q in range(2)]
        csx1 = sb("csx_l1", [P, 1], F32, L0)
        s2c = sb("s2c", [P, NT], F32, L0)
        s2p = sb("s2p", [P, NT], F32, L0)
        smax = sb("smax", [P, 4], F32, L0)
        bd = [sb(f"bd{q}", [P, 3 * NT], F32, L0) for q in range(2)]
        adj_in = [Pt[0][:, s, :].bitcast(I32) for s in range(4)]
        Gi = [Pt[0][:, 4 + s, 0:N // 2].bitcast(BF16) for s in range(2)]
        wraw = Pt[1][:, 0, 0:P]
        woraw = Pt[1][:, 0, P:2 * P]
        asb = Pt[1][:, 1, 0:D]
        adb = Pt[1][:, 1, D:2 * D]
        wprod = Pt[1][:, 2, 0:2 * D]
        w0T = Pt[1][:, 3, 0:P]
        a1c = Pt[1][:, 4, 0:2]
        a1r = Pt[1][:, 4, P:2 * P]
        L0.close()

        L1 = ctx
        C = [sb(f"C{q}", [P, NT, N], U8, L1) for q in range(2)]
        Hm = [sb(f"Hm{q}", [P, NT, N], FP8, L1) for q in range(2)]
        srow = [sb(f"srow{q}", [P, N], F32, L1) for q in range(4)]
        V = [sb(f"V{q}", [P, NT, VW, 3], F32, L1) for q in range(4)]
        BD = sb("BD", [P, NT, NH, 2], F32, L1)
        R1 = sb("R1", [P, NT, NH], F32, L1)
        m64 = sb("m64", [P, NH], F32, L1)
        M64 = sb("M64", [P, NH], F32, L1)
        edp = sb("edp", [P, NT, NH], F32, L1)
        esm = sb("esm", [P, NT, NH], F32, L1)
        cmps = sb("cmps", [P, NH, 2, NT], F32, L1)
        cmph = [sb(f"cmph{q}", [P, 2, NT], F32, L1) for q in range(4)]
        Dexp = sb("Dexp", [P, NT, NH], F32, L1)
        csum3 = sb("csum3", [P, NH, VW, 3], F32, L1)
        Sb = sb("Sb", [P, NT, H, VW], F32, L1)
        hc = sb("hc", [P, NT, D], F32, L1)
        hT = sb("hT", [P, N], F32, L1)
        xres = sb("xres", [P, NT, D], F32, L1)
        yout = sb("yout", [P, NT, D], F32, L1)

        XT = ctx.enter_context(nc.psum_tensor("XT", [P, 1024], F32))
        HH = ctx.enter_context(nc.psum_tensor("HH", [P, 3, 512], F32))
        OUT = ctx.enter_context(nc.psum_tensor("OUT", [P, 3, 512], F32))
        cs0_ps = HH[0:1, 2, 258:386]
        cs1_ps = HH[0:1, 2, 300:428]
        acc = [HH[:, 0:2, :], OUT[:, 0:2, :]]
        TP = XT
        OPb = [HH[:, 2, :], OUT[:, 2, :]]

        def third(t, w):
            return [(t[:, 0:2, 0:3 * w].rearrange("p k (t w) -> p k t w", w=w), 0, 6),
                    (t[:, 2, 0:2 * w].rearrange("p (t w) -> p t w", w=w), 6, 8)]

        adj_ld = [sem(f"adj_ld{s}") for s in range(4)]
        w_ld, const_ok = sem("w_ld"), sem("const_ok")
        gi_ok, gT_ps, gt_ok, gtn_ok = sem("gi_ok"), sem("gT_ps"), sem("gt_ok"), sem("gtn_ok")
        deg_ps, empty_ok = sem("deg_ps"), sem("empty_ok")
        wT_ps, wT_ok, wa_ps, w_ok = sem("wT_ps"), sem("wT_ok"), sem("wa_ps"), sem("w_ok")
        lp_lnk, set_lnk = sem("lp_lnk"), sem("set_lnk")
        xin_ld = [sem(f"xin_ld{q}") for q in range(2)]
        xr0_ld = [sem(f"xr0_ld{q}") for q in range(2)]
        xT_ps, xT_ok, h_ps, s1_ps = sem("xT_ps"), sem("xT_ok"), sem("h_ps"), sem("s1_ps")
        h_ok, mx_ok, gmx_ok, s2_ok, bd_lnk, R_ok = [sem(n) for n in
            ("h_ok", "mx_ok", "gmx_ok", "s2_ok", "bd_lnk", "R_ok")]
        relu_ok, P_ok, out_ps, out_rd, min_ok, elu_ok = [sem(n) for n in
            ("relu_ok", "P_ok", "out_ps", "out_rd", "min_ok", "elu_ok")]
        mv_ok, rs_ok, x1_ok, x1_st, x1T_ps, x1T_ok = [sem(n) for n in
            ("mv_ok", "rs_ok", "x1_ok", "x1_st", "x1T_ps", "x1T_ok")]
        xp_ps, xp_ok, ed_ok, es_ps, es_ok, es_st = [sem(n) for n in
            ("xp_ps", "xp_ok", "ed_ok", "es_ps", "es_ok", "es_st")]
        f_lnk, m_lnk, pf_lnk, pm_lnk = sem("f_lnk"), sem("m_lnk"), sem("pf_lnk"), sem("pm_lnk")
        ed_mx, ed_gmx, edp_ok, bexp_ok, head_ok, c3_lnk, z_lnk = [sem(n) for n in
            ("ed_mx", "ed_gmx", "edp_ok", "bexp_ok", "head_ok", "c3_lnk", "z_lnk")]
        srow_ld = [sem(f"srow_ld{q}") for q in range(4)]
        V_ok, v_lnk, ccmp_a, ccmp_v, hm_ok, hd_ps, red_ok = [sem(n) for n in
            ("V_ok", "v_lnk", "ccmp_a", "ccmp_v", "hm_ok", "hd_ps", "red_ok")]
        hc_ok, hT_ps, hT_ok, op_ps, op_rd, y_ok, y_st, xres_ld = [sem(n) for n in
            ("hc_ok", "hT_ps", "hT_ok", "op_ps", "op_rd", "y_ok", "y_st", "xres_ld")]
        k_lnk, t_lnk, mv1_ok, rs1_ok, pt_lnk = [sem(n) for n in ("k_lnk", "t_lnk", "mv1_ok", "rs1_ok", "pt_lnk")]

        x_t = x.rearrange("b (t p) d -> b p t d", p=P)
        x1_t = x1_dram.rearrange("b (t p) d -> b p t d", p=P)
        out_t = out.rearrange("b (t p) d -> b p t d", p=P)
        adj_t = adj.rearrange("(t p) j -> t p j", p=P)
        N_W = 8

        def l0_steps(eng, body):
            body(0, 0, 0)
            with eng.Fori(0, (BS - 2) // 2) as t:
                body(t * 2 + 1, 1, t)
                body(t * 2 + 2, 0, t + 1)
            body(BS - 1, 1, BS // 2 - 1)

        def is_first(b):
            return isinstance(b, int) and b == 0

        def is_last(b):
            return isinstance(b, int) and b == BS - 1

        block = ctx.enter_context(nc.Block())

        @block.sync
        def _(sp):
            sp.dma_start(wraw, w0).then_inc(w_ld, 16)
            sp.dma_start(W1[:, 0:D].rearrange("d (h f) -> d h f", h=H),
                         w1.rearrange("h d f -> d h f")).then_inc(w_ld, 16)
            for k in range(2):
                sp.dma_start(a1c[:, k:k + 1], a0[k * P:(k + 1) * P, :]).then_inc(w_ld, 16)
            sp.dma_start(asb, a_src.rearrange("h f -> (h f)").partition_broadcast(P)).then_inc(w_ld, 16)
            sp.dma_start(adb, a_dst.rearrange("h f -> (h f)").partition_broadcast(P)).then_inc(w_ld, 16)
            sp.dma_start(woraw, w_out).then_inc(w_ld, 16)
            sp.dma_start(lp[:], beta.partition_broadcast(P)).then_inc(w_ld, 16)
            for t in range(NT):
                if t >= 4:
                    sp.wait_ge(gi_ok, t - 3)
                sp.dma_start(adj_in[t % 4], adj_t[t]).then_inc(adj_ld[t % 4], 16)
            for q in range(2):
                sp.dma_start(xin[q][:], x_t[q]).then_inc(xin_ld[q], 16)
                sp.dma_start(xres0[q][:], x_t[q]).then_inc(xr0_ld[q], 16)

            def load_in(b, q):
                sp.wait_ge(xT_ps, b + 1)
                sp.dma_start(xin[q][:], x_t[bass.ds(b + 2, 1)].rearrange("o p t d -> (o p) t d")
                             if not isinstance(b, int) else x_t[b + 2]).then_inc(xin_ld[q], 16)

            def load_res(b, q):
                sp.dma_start(xres0[q][:], x_t[bass.ds(b + 2, 1)].rearrange("o p t d -> (o p) t d")
                             if not isinstance(b, int) else x_t[b + 2]).then_inc(xr0_ld[q], 16)

            def store_es(b):
                sp.wait_ge(es_ok, b + 1)
                sp.dma_start(es_dram[bass.ds(b * H, H), :], es_row[:]).then_inc(es_st, 16)

            def store_x1(b):
                sp.wait_ge(x1_ok, b + 1)
                sp.dma_start(x1_t[bass.ds(b, 1)].rearrange("o p t d -> (o p) t d")
                             if not isinstance(b, int) else x1_t[b], x1b[:]).then_inc(x1_st, 16)

            load_in(0, 0)
            store_x1(0)
            load_res(0, 0)
            with sp.Fori(0, 2) as t:
                for b, q in ((t * 2 + 1, 1), (t * 2 + 2, 0)):
                    load_in(b, q)
                    store_es(b - 1)
                    store_x1(b)
                    load_res(b, q)
            load_in(5, 1)
            store_es(4)
            store_x1(5)
            load_res(5, 1)
            for b in (6, 7):
                store_es(b - 1)
                store_x1(b)
            store_es(7)
            sp.wait_ge(es_st, 16 * BS)
            sp.wait_ge(x1_st, 16 * BS)
            sp.wait_ge(head_ok, 1)

            def load_row(b, h):
                n = b * H + h
                if not (isinstance(b, int) and n < 4):
                    sp.wait_ge(ccmp_a, n - 3)
                    sp.wait_ge(ccmp_v, n - 3)
                sp.dma_start(srow[h % 4][:], es_dram[bass.ds(n, 1), :].rearrange("o n -> (o n)")
                             .partition_broadcast(P)).then_inc(srow_ld[h % 4], 16)
                sp.dma_start(cmph[h % 4][:].rearrange("p k t -> p (k t)"),
                             cmps[:, bass.ds(n, 1), :, :].rearrange("p o k t -> p (o k t)")).then_inc(srow_ld[h % 4], 16)

            def l1_batch(b):
                for h in range(H):
                    load_row(b, h)
                    if h == 5:
                        if not is_first(b):
                            sp.wait_ge(y_ok, b)
                            sp.dma_start(out_t[b - 1] if isinstance(b, int) else
                                         out_t[bass.ds(b - 1, 1)].rearrange("o p t d -> (o p) t d"),
                                         yout[:]).then_inc(y_st, 16)
                        sp.dma_start(xres[:], x1_t[b] if isinstance(b, int) else
                                     x1_t[bass.ds(b, 1)].rearrange("o p t d -> (o p) t d")).then_inc(xres_ld, 16)

            l1_batch(0)
            with sp.Fori(1, BS) as b:
                l1_batch(b)
            sp.wait_ge(y_ok, BS)
            sp.dma_start(out_t[BS - 1], yout[:]).then_inc(y_st, 16)
            sp.wait_ge(y_st, 16 * BS)

        @block.gpsimd
        def _(pool):
            pool.memset(ident[:], 0.0).then_inc(set_lnk, 1)
            pool.wait_ge(set_lnk, 1)
            pool.affine_select(out=ident[:], in_=ident[:], compare_op=ALU.not_equal, fill=1.0, base=0,
                               pattern=[[-1, P]], channel_multiplier=1).then_inc(set_lnk, 1)
            pool.wait_ge(set_lnk, 2)
            pool.tensor_copy(identb[:], ident[:])
            pool.memset(ones_col[:], 1.0)
            pool.memset(lneps[:], LN_EPS)
            pool.memset(mhalf[:], -0.5)
            pool.memset(rslope[:], 1.0 - SLOPE)
            pool.memset(emptyf[:], 0.0)
            pool.memset(emptyb[:], 0.0)
            for q in range(2):
                pool.memset(crow0[q][:], 0.0).then_inc(set_lnk, 1)
            pool.wait_ge(set_lnk, 4)
            for q in range(2):
                pool.memset(crow0[q][0:1, D:D + 1], float(N))
                pool.memset(hA[q][:, :, D:D + 1], 1.0)
            pool.memset(tiny[:], 0.0).then_inc(const_ok, 1)

            pf = Links(pool, pf_lnk, 1)
            pm = Links(pool, pm_lnk, 1)

            def front(b):
                pf.begin(b)
                pool.wait_ge(mx_ok, b + 1)
                if not is_first(b):
                    pool.wait_ge(R_ok, b)
                pool.tensor_tensor(idle[:], lneps[:, 0:1], lneps[:, 0:1], ALU.add)
                pf.link(pool.partition_all_reduce(smax[:, 1:2], smax[:, 0:1], P, RMAX))
                pool.tensor_tensor(smax[:, 2:3], smax[:, 1:2], rslope[:], ALU.mult).then_inc(gmx_ok, 1)
                pf.end()

            def rsqrt(links, b, ready, done):
                links.begin(b)
                pool.wait_ge(ready, b + 1)
                links.link(pool.tensor_tensor(rstd_e[:], mv[:, :, 1], lneps[:], ALU.add))
                pool.tensor_tensor(rstd[:], rstd_e[:], mhalf[:], ALU.pow).then_inc(done, 1)
                links.end()

            front(0)

            def step(b, q, _):
                if not is_last(b):
                    front(b + 1)
                rsqrt(pm, b, mv_ok, rs_ok)
            l0_steps(pool, step)

            pool.wait_ge(ed_mx, 1)
            pool.partition_all_reduce(M64[:], m64[:], P, RMAX).then_inc(ed_gmx, 1)
            pool.memset(csum3[:], 0.0).then_inc(ed_gmx, 1)
            pool.wait_ge(head_ok, 1)

            vl = Links(pool, v_lnk, 2)

            def values(b, h):
                n = b * H + h
                vl.begin(n)
                if not (isinstance(b, int) and n < 4):
                    pool.wait_ge(hd_ps, n - 3)
                v = V[h % 4]
                bdn = BD[:, :, bass.ds(n, 1), :].rearrange("p t o k -> p t (o k)")
                f0 = bass.ds(b * D + h * DH, DH)
                vk = v[:, :, :, 0].rearrange("p t (k f) -> p t k f", k=2)
                for k in range(2):
                    pool.tensor_tensor(vk[:, :, k, 0:DH], xp[:, :, f0],
                                       bdn[:, :, k:k + 1].to_broadcast([P, NT, DH]), ALU.mult)
                vl.link(pool.tensor_copy(vk[:, :, :, DH:KW].rearrange("p t k o -> p t (k o)"), bdn))
                hi = v[:].bitcast(BF16).rearrange("p t f (k u) -> p (t f) k u", u=2)[:, :, :, 1]
                w = v[:].rearrange("p t f k -> p (t f) k")
                vl.link(pool.tensor_tensor(w[:, :, 1], w[:, :, 0], hi[:, :, 0], ALU.subtract))
                pool.tensor_tensor(w[:, :, 2], w[:, :, 1], hi[:, :, 1], ALU.subtract).then_inc(V_ok, 1)
                vl.end()

            pt = Links(pool, pt_lnk, 1)

            def l1_batch(b):
                for h in range(H):
                    values(b, h)
                    if h == 5 and not is_first(b):
                        rsqrt(pt, b - 1, mv1_ok, rs1_ok)
            l1_batch(0)
            with pool.Fori(1, BS) as b:
                l1_batch(b)
            rsqrt(pt, BS - 1, mv1_ok, rs1_ok)

        @block.scalar
        def _(act):
            a = nc.scalar
            act.wait_ge(w_ld, 16 * N_W)
            act.wait_ge(const_ok, 1)

            def chain(ins, k):
                ins.then_inc(lp_lnk, 1)
                act.wait_ge(lp_lnk, k)
            chain(a.activation(tiny[:, 0:1], lp[:], ACT.Abs), 1)
            chain(a.activation(tiny[:, 1:2], tiny[:, 0:1], ACT.Exp, scale=-1.0), 2)
            chain(a.activation(tiny[:, 2:3], tiny[:, 1:2], ACT.Ln, bias=1.0), 3)
            chain(a.activation(tiny[:, 3:4], lp[:], ACT.Relu, bias=0.0), 4)
            chain(a.activation(tiny[:, 5:6], tiny[:, 4:5], ACT.Ln, bias=1.0 + LOG_EPS), 5)

            for t in range(NT):
                act.wait_ge(gt_ok, t + 1)
                a.activation(GtN[:, :, t * P:(t + 1) * P], Gt[:, :, t * P:(t + 1) * P], ACT.Copy,
                             scale=-1.0, saturate=False).then_inc(gtn_ok, 1)

            bdl = Links(act, bd_lnk, 3)

            def front(b, q):
                act.wait_ge(xT_ps, b + 1)
                a.activation(xT[:], XT[:], ACT.Copy, accum_out=csx[q][:]).then_inc(xT_ok, 1)
                act.wait_ge(mx_ok, b + 1)
                for v, t0, t1 in third(HH, D + 1):
                    last = a.activation(hA[q][:, t0:t1, 0:D] if t0 else
                                        hA[q][:, t0:t1, 0:D].rearrange("p (k t) d -> p k t d", k=2),
                                        v[..., 0:D], ACT.Copy)
                last.then_inc(h_ok, 1)
                act.wait_ge(s2_ok, b + 1)
                bdl.begin(b)
                bdl.link(a.activation(bd[q][:, 0:NT], s2p[:], ACT.Exp))
                bdl.link(a.activation(bd[q][:, NT:2 * NT], s2p[:], ACT.Exp, scale=SLOPE))
                bdl.link(a.activation(bd[q][:, 2 * NT:], bd[q][:, NT:2 * NT], ACT.Copy, scale=-1.0))
                bdl.end()
                act.wait_ge(s1_ps, b + 1)
                act.wait_ge(gmx_ok, b + 1)
                a.activation(Rb[:], XT[:], ACT.Exp, scale=1.0 - SLOPE, bias=smax[:, 2:3]).then_inc(R_ok, 1)

            def scores(b, q):
                act.wait_ge(R_ok, b + 1)
                if not (isinstance(b, int) and b < 2):
                    act.wait_ge(out_ps, b - 1)
                for c in range(NT):
                    a.activation(Pt[q][:, c, :], Rb[:], ACT.Relu, scale=bd[q][:, c:c + 1],
                                 bias=bd[q][:, 2 * NT + c:2 * NT + c + 1]).then_inc(relu_ok, 1)

            def proj(b):
                act.wait_ge(x1T_ps, b + 1)
                a.activation(x1T[:], XT[:], ACT.Copy, accum_out=csx1[:]).then_inc(x1T_ok, 1)
                act.wait_ge(ed_ok, b + 1)
                for v, t0, t1 in third(HH, D + 2 * H):
                    o = xp[:, t0:t1, bass.ds(b * D, D)]
                    last = a.activation(o if t0 else o.rearrange("p (k t) d -> p k t d", k=2),
                                        v[..., 0:D], ACT.Copy)
                last.then_inc(xp_ok, 1)

            def step(b, q, _):
                if not is_last(b):
                    front(b + 1, 1 - q)
                    scores(b + 1, 1 - q)
                if not is_first(b):
                    proj(b - 1)
                act.wait_ge(min_ok, b + 1)
                a.activation(et[:], et[:], ACT.Exp).then_inc(elu_ok, 1)

            front(0, 0)
            act.wait_ge(w_ok, 1)
            act.wait_ge(gt_ok, NT)
            scores(0, 0)
            l0_steps(act, step)
            proj(BS - 1)

            act.wait_ge(edp_ok, 1)
            a.activation(BD[:, :, :, 0], edp[:], ACT.Exp, bias=lp[:])
            a.activation(Dexp[:], edp[:], ACT.Exp, scale=SLOPE, bias=lp[:])
            a.activation(R1[:], esm[:], ACT.Exp, scale=1.0 - SLOPE).then_inc(bexp_ok, 1)
            act.wait_ge(head_ok, 1)

            def compare(b, h):
                n = b * H + h
                act.wait_ge(srow_ld[h % 4], (b * 2 + h // 4 + 1) * 32)
                if not (isinstance(b, int) and n < 2):
                    act.wait_ge(hm_ok, n - 1)
                for c in range(AC):
                    last = a.activation(C[h % 2][:, c, :], srow[h % 4][:], ACT.Sigmoid, scale=STEEP,
                                        bias=cmph[h % 4][:, 0, c:c + 1])
                last.then_inc(ccmp_a, 1)

            def copy_hT(b):
                act.wait_ge(hT_ps, b + 1)
                a.activation(hT[:], TP[:], ACT.Copy).then_inc(hT_ok, 1)

            def l1_batch(b):
                for h in range(H):
                    compare(b, h)
                    if h == 3 and not is_first(b):
                        copy_hT(b - 1)
            l1_batch(0)
            with act.Fori(1, BS) as b:
                l1_batch(b)
            copy_hT(BS - 1)

        @block.vector
        def _(dve):
            v = nc.vector
            dve.wait_ge(const_ok, 1)
            dve.wait_ge(w_ld, 16 * N_W)
            for k, (vec, col) in enumerate(((adb, D), (asb, D + H))):
                v.tensor_tensor(wprod[:, k * D:(k + 1) * D], W1[:, 0:D], vec, ALU.mult)
            v.tensor_copy(a1r, a1c[:, 0:1].to_broadcast([P, P])).then_inc(z_lnk, 1)
            dve.wait_ge(z_lnk, 1)
            v.tensor_reduce(W1[:, D:D + 2 * H], wprod.rearrange("p (h f) -> p h f", f=DH), AX.X, ALU.add)
            dve.wait_ge(wT_ps, 1)
            v.tensor_copy(w0T, XT[:, 0:P])
            v.tensor_copy(WoT[:], XT[:, P:2 * P])
            v.tensor_copy(W0[:, 0:D], wraw).then_inc(wT_ok, 1)
            dve.wait_ge(wa_ps, 1)
            v.tensor_copy(Wa1[:], XT[:, 2 * P:3 * P])
            v.tensor_copy(W0[:, D:D + 1], XT[:, 3 * P:3 * P + 1]).then_inc(z_lnk, 1)
            dve.wait_ge(lp_lnk, 5)
            v.tensor_tensor(tiny[:, 6:7], tiny[:, 2:3], tiny[:, 3:4], ALU.add).then_inc(z_lnk, 1)
            dve.wait_ge(z_lnk, 3)
            v.tensor_tensor(lp[:], tiny[:, 6:7], tiny[:, 5:6], ALU.mult).then_inc(w_ok, 1)
            def mask_copy(t):
                dve.wait_ge(gT_ps, t + 1)
                v.tensor_copy(Gt[:, :, t * P:(t + 1) * P],
                              OUT[:, t % 2, :].bitcast(BF16).rearrange("p (c i) -> p c i", c=NT), saturate=False).then_inc(gt_ok, 1)

            for t in range(NT):
                dve.wait_ge(adj_ld[t % 4], 16 * (t // 4 + 1))
                if t >= 2:
                    dve.wait_ge(gT_ps, t - 1)
                v.tensor_scalar(Gi[t % 2], adj_in[t % 4], 0, EDGE, ALU.is_gt, ALU.mult).then_inc(gi_ok, 1)
                if t >= 1:
                    mask_copy(t - 1)
            mask_copy(NT - 1)
            dve.wait_ge(deg_ps, 1)
            v.tensor_scalar(emptyf[0:1, :], XT[0:1, :], 0.0, float(EDGE_BYTE), ALU.is_equal, ALU.mult)
            v.tensor_scalar(emptyb[0:1, :], XT[0:1, :], 0.0, EDGE, ALU.is_equal, ALU.mult).then_inc(empty_ok, 1)

            fl = Links(dve, f_lnk, 1)
            ml = Links(dve, m_lnk, 4)

            def front(b, q):
                fl.begin(b)
                dve.wait_ge(h_ps, b + 1)
                if not is_first(b):
                    dve.wait_ge(gmx_ok, b)
                for hv, t0, t1 in third(HH, D + 1):
                    s = s2c[:, t0:t1]
                    last = v.tensor_copy(s if t0 else s.rearrange("p (k t) -> p k t", k=2), hv[..., D])
                if not (isinstance(b, int) and b < 2):
                    dve.wait_ge(out_ps, b - 1)
                fl.link(v.tensor_copy(crow0[q][0:1, 0:D], cs0_ps))
                v.tensor_reduce(smax[:, 0:1], s2c[:], AX.X, ALU.max).then_inc(mx_ok, 1)
                dve.wait_ge(gmx_ok, b + 1)
                if not is_first(b):
                    dve.wait_ge(R_ok, b)
                v.tensor_scalar(s2p[:], s2c[:], smax[:, 1:2], None, ALU.subtract).then_inc(s2_ok, 1)
                fl.end()

            def scores(b, q):
                for c in range(NT):
                    dve.wait_ge(relu_ok, b * NT + c + 1)
                    v.scalar_tensor_tensor(Pt[q][:, c, :], Pt[q][:, c, :], bd[q][:, NT + c:NT + c + 1],
                                           Gt[:, c, :].bitcast(U8), ALU.add, ALU.mult).then_inc(P_ok, 1)

            def layernorm_stats(links, y, done):
                for t in range(NT):
                    last = v.bn_stats(stats[:, t, :], y[:, t, :])
                links.link(last)
                v.tensor_copy(idle_v[:], lneps[:, 0:1])
                for t in range(NT):
                    last = v.bn_aggr(mv[:, t, :], stats[:, t, :])
                last.then_inc(done, 1)

            def layernorm_scale(dst, y):
                for t in range(NT):
                    last = v.tensor_scalar(dst[:, t, :], y[:, t, :], mv[:, t, 0:1], rstd[:, t:t + 1],
                                           ALU.subtract, ALU.mult)
                return last

            def finish(b, q, half):
                ml.begin(b)
                dve.wait_ge(out_ps, b + 1)
                for o, t0, t1 in third(OUT, D + 1):
                    r = rden[:, t0:t1]
                    last = v.reciprocal(r if t0 else r.rearrange("p (k t) -> p k t", k=2), o[..., D])
                ml.link(last)
                for o, t0, t1 in third(OUT, D + 1):
                    if t0:
                        last = v.tensor_tensor(hp[:, t0:t1, :], o[..., 0:D],
                                               rden[:, t0:t1].unsqueeze(2).to_broadcast([P, t1 - t0, D]), ALU.mult)
                    else:
                        v.tensor_tensor(hp[:, 0:6, :].rearrange("p (k t) d -> p k t d", k=2), o[..., 0:D],
                                        rden[:, 0:6].rearrange("p (k t) -> p k t", k=2).unsqueeze(3)
                                        .to_broadcast([P, 2, 3, D]), ALU.mult)
                last.then_inc(out_rd, 1)
                dve.wait_ge(out_rd, b + 1)
                v.tensor_scalar(et[:], hp[:], 0.0, None, ALU.min).then_inc(min_ok, 1)
                dve.wait_ge(xr0_ld[q], (half + 1) * 16)
                ml.link(v.scalar_tensor_tensor(hp[:], hp[:], 0.0, xres0[q][:], ALU.max, ALU.add))
                dve.wait_ge(elu_ok, b + 1)
                ml.link(v.scalar_tensor_tensor(hp[:], et[:], -1.0, hp[:], ALU.add, ALU.add))
                layernorm_stats(ml, hp, mv_ok)
                dve.wait_ge(rs_ok, b + 1)
                if not is_first(b):
                    dve.wait_ge(x1_st, b * 16)
                    dve.wait_ge(x1T_ps, b)
                layernorm_scale(x1b, hp).then_inc(x1_ok, 1)
                ml.end()

            def proj(b):
                dve.wait_ge(xp_ps, b + 1)
                for hv, t0, t1 in third(HH, D + 2 * H):
                    for k in range(2):
                        o = edes[:, t0:t1, k, bass.ds(b * H, H)]
                        last = v.tensor_copy(o if t0 else o.rearrange("p (k t) h -> p k t h", k=2),
                                             hv[..., D + k * H:D + (k + 1) * H])
                v.tensor_copy(csum1[0:1, bass.ds(b * D, D)], cs1_ps).then_inc(ed_ok, 1)
                dve.wait_ge(es_ps, b + 1)
                if not is_first(b):
                    dve.wait_ge(es_st, b * 16)
                v.tensor_copy(es_row[:], XT[0:H, :]).then_inc(es_ok, 1)

            def step(b, q, half):
                if not is_last(b):
                    front(b + 1, 1 - q)
                    scores(b + 1, 1 - q)
                if not is_first(b):
                    proj(b - 1)
                finish(b, q, half)

            front(0, 0)
            scores(0, 0)
            l0_steps(dve, step)
            proj(BS - 1)

            dve.wait_ge(ed_ok, BS)
            dve.wait_ge(es_ok, BS)
            dve.wait_ge(out_ps, BS)
            dve.wait_ge(es_st, 16 * BS)
            v.tensor_reduce(m64[:], edes[:, :, 0, :].rearrange("p t e -> p e t"), AX.X, ALU.max).then_inc(ed_mx, 1)
            edn = edes[:, :, 0, :].rearrange("p t e -> p e t")
            v.tensor_scalar(cmps[:, :, 0, :], edn, STEEP, None, ALU.mult)
            v.tensor_scalar(cmps[:, :, 1, :], edn, -1.0, None, ALU.mult)
            dve.wait_ge(ed_gmx, 2)
            mb = M64[:].unsqueeze(1).to_broadcast([P, NT, NH])
            v.tensor_tensor(edp[:], edes[:, :, 0, :], mb, ALU.subtract)
            v.tensor_tensor(esm[:], edes[:, :, 1, :], mb, ALU.add).then_inc(edp_ok, 1)
            cs = csum3[0:1, :, KW:VW, :]
            csh = cs.bitcast(BF16)
            v.tensor_copy(cs[:, :, 0:DH, 0], csum1[:].rearrange("p (e f) -> p e f", f=DH))
            v.memset(cs[:, :, DH, 0], float(N)).then_inc(c3_lnk, 1)
            dve.wait_ge(c3_lnk, 1)
            v.tensor_tensor(cs[:, :, :, 1], cs[:, :, :, 0], csh[:, :, :, 1], ALU.subtract).then_inc(c3_lnk, 1)
            dve.wait_ge(c3_lnk, 2)
            v.tensor_tensor(cs[:, :, :, 2], cs[:, :, :, 1], csh[:, :, :, 3], ALU.subtract)
            dve.wait_ge(bexp_ok, 1)
            v.tensor_scalar(BD[:, :, :, 1], Dexp[:], -1.0, None, ALU.mult).then_inc(head_ok, 1)
            dve.wait_ge(head_ok, 1)

            kl = Links(dve, k_lnk, 3)
            tl = Links(dve, t_lnk, 1)

            def compare(b, h):
                n = b * H + h
                dve.wait_ge(srow_ld[h % 4], (b * 2 + h // 4 + 1) * 32)
                if not (isinstance(b, int) and n < 2):
                    dve.wait_ge(hm_ok, n - 1)
                for c in range(AC, NT):
                    last = v.tensor_scalar(C[h % 2][:, c, :], srow[h % 4][:], cmph[h % 4][:, 1, c:c + 1], None,
                                           ALU.is_gt)
                last.then_inc(ccmp_v, 1)

            def mask(b, h):
                n = b * H + h
                dve.wait_ge(ccmp_a, n + 1)
                dve.wait_ge(ccmp_v, n + 1)
                if not (isinstance(b, int) and n < 2):
                    dve.wait_ge(hd_ps, n - 1)
                v.scalar_tensor_tensor(Hm[h % 2][:].rearrange("p t n -> p (t n)").bitcast(I32),
                                       C[h % 2][:].rearrange("p t n -> p (t n)").bitcast(I32), EDGE_SHIFT,
                                       Gt[:].rearrange("p t n -> p (t n)").bitcast(I32),
                                       ALU.logical_shift_left, ALU.bitwise_and).then_inc(hm_ok, 1)

            def parts(b, h):
                n = b * H + h
                dve.wait_ge(hd_ps, n + 1)
                if h == 0 and not is_first(b):
                    dve.wait_ge(hc_ok, b)
                v.tensor_reduce(Sb[:, :, h, :].rearrange("p (k t) c -> p k t c", k=2),
                                acc[h % 2][:, :, 0:4 * VW * 3].rearrange("p k (t c s) -> p k t c s", s=3, c=VW),
                                AX.X, ALU.add).then_inc(red_ok, 1)

            def combine(b):
                kl.begin(b)
                dve.wait_ge(red_ok, (b + 1) * H)
                if not is_first(b):
                    dve.wait_ge(hT_ps, b)
                r = R1[:, :, bass.ds(b * H, H)].unsqueeze(3).to_broadcast([P, NT, H, KW])
                kl.link(v.tensor_tensor(Sb[:, :, :, 0:KW], Sb[:, :, :, 0:KW], r, ALU.mult))
                kl.link(v.tensor_tensor(Sb[:, :, :, 0:KW], Sb[:, :, :, 0:KW], Sb[:, :, :, KW:VW], ALU.add))
                kl.link(v.reciprocal(rden[:].rearrange("p (t h) -> p t h", h=H), Sb[:, :, :, DH]))
                v.tensor_tensor(hc[:].rearrange("p t (h f) -> p t h f", h=H), Sb[:, :, :, 0:DH],
                                rden[:].rearrange("p (t h) -> p t h", h=H).unsqueeze(3)
                                .to_broadcast([P, NT, H, DH]), ALU.mult).then_inc(hc_ok, 1)
                kl.end()

            def finish1(b):
                tl.begin(b)
                dve.wait_ge(op_ps, b + 1)
                dve.wait_ge(xres_ld, (b + 1) * 16)
                if not is_first(b):
                    dve.wait_ge(y_st, b * 16)
                for k in range(2):
                    last = v.tensor_tensor(yout[:, 4 * k:4 * k + 4, :], OPb[k].rearrange("p (t d) -> p t d", d=D),
                                           xres[:, 4 * k:4 * k + 4, :], ALU.add)
                last.then_inc(op_rd, 1)
                dve.wait_ge(op_rd, b + 1)
                layernorm_stats(tl, yout, mv1_ok)
                dve.wait_ge(rs1_ok, b + 1)
                layernorm_scale(yout, yout).then_inc(y_ok, 1)
                tl.end()

            def l1_batch(b):
                for h in range(1, H + 1):
                    bb, hh = (b, h) if h < H else (b + 1, 0)
                    if not (is_last(b) and h == H):
                        if not (is_last(b) and h == H - 1):
                            compare(*((bb, hh + 1) if hh + 1 < H else (b + 1, 0)))
                        mask(bb, hh)
                    parts(b, h - 1)
                    if h == 4 and not is_first(b):
                        finish1(b - 1)
                combine(b)

            compare(0, 0)
            compare(0, 1)
            mask(0, 0)
            l1_batch(0)
            with dve.Fori(1, BS - 1) as b:
                l1_batch(b)
            l1_batch(BS - 1)
            finish1(BS - 1)

        @block.tensor
        def _(pe):
            mm = nc.tensor.matmul
            pe.wait_ge(const_ok, 1)
            pe.wait_ge(w_ld, 16 * N_W)
            nc.tensor.transpose(XT[:, 0:P], wraw, ident[:])
            nc.tensor.transpose(XT[:, P:2 * P], woraw, ident[:]).then_inc(wT_ps, 1)
            pe.wait_ge(wT_ok, 1)
            mm(XT[:, 2 * P:3 * P], w0T, a1r, start=True, stop=True)
            mm(XT[:, 3 * P:3 * P + 1], w0T, a1c[:, 1:2], start=True, stop=True).then_inc(wa_ps, 1)
            for t in range(NT):
                pe.wait_ge(gi_ok, t + 1)
                if t >= 2:
                    pe.wait_ge(gt_ok, t - 1)
                for c in range(NT):
                    last = nc.tensor.transpose(OUT[:, t % 2, :].bitcast(BF16)[:, c * P:(c + 1) * P],
                                               Gi[t % 2][:, c * P:(c + 1) * P], identb[:])
                last.then_inc(gT_ps, 1)
            pe.wait_ge(gt_ok, NT)
            pe.wait_ge(w_ok, 1)
            for k in range(2):
                for c in range(NT):
                    last = mm(XT[0:1, k * 512:(k + 1) * 512], ones_col[:], Gt[:, c, k * 512:(k + 1) * 512],
                              start=c == 0, stop=c == NT - 1)
            last.then_inc(deg_ps, 1)
            pe.wait_ge(empty_ok, 1)

            def tile(t, ps, w):
                return ps[:, t // 3, (t % 3) * w:(t % 3 + 1) * w]

            def front(b, q, half):
                pe.wait_ge(xin_ld[q], (half + 1) * 16)
                if not (isinstance(b, int) and b < 3):
                    pe.wait_ge(es_ok, b - 2)
                    pe.wait_ge(xp_ok, b - 2)
                if not is_first(b):
                    pe.wait_ge(R_ok, b)
                    pe.wait_ge(h_ok, b)
                for t in range(NT):
                    last = nc.tensor.transpose(XT[:, t * P:(t + 1) * P], xin[q][:, t, :], ident[:])
                last.then_inc(xT_ps, 1)
                pe.wait_ge(xT_ok, b + 1)
                mm(cs0_ps, csx[q][:], W0[:, 0:D], start=True, stop=True)
                for t in range(NT):
                    last = mm(tile(t, HH, D + 1), xT[:, t * P:(t + 1) * P], W0[:], start=True, stop=True)
                last.then_inc(h_ps, 1)
                for k in range(2):
                    last = mm(XT[:, k * 512:(k + 1) * 512], Wa1[:], xT[:, k * 512:(k + 1) * 512],
                              start=True, stop=True)
                last.then_inc(s1_ps, 1)

            def products(b, q):
                pe.wait_ge(P_ok, (b + 1) * NT)
                pe.wait_ge(h_ok, b + 1)
                if not is_first(b):
                    pe.wait_ge(out_rd, b)
                for t in range(NT):
                    o = tile(t, OUT, D + 1)
                    for c in range(NT):
                        mm(o, Pt[q][:, c, t * P:(t + 1) * P], hA[q][:, c, :], start=c == 0, stop=False)
                    last = mm(o, emptyf[:, t * P:(t + 1) * P], crow0[q][:], start=False, stop=True)
                last.then_inc(out_ps, 1)

            def proj(b, fronts):
                pe.wait_ge(x1_ok, b + 1)
                pe.wait_ge(R_ok, fronts)
                pe.wait_ge(h_ok, fronts)
                pe.wait_ge(mx_ok, fronts)
                for t in range(NT):
                    last = nc.tensor.transpose(XT[:, t * P:(t + 1) * P], x1b[:, t, :], ident[:])
                last.then_inc(x1T_ps, 1)
                pe.wait_ge(x1T_ok, b + 1)
                mm(cs1_ps, csx1[:], W1[:, 0:D], start=True, stop=True)
                for t in range(NT):
                    last = mm(tile(t, HH, D + 2 * H), x1T[:, t * P:(t + 1) * P], W1[:], start=True, stop=True)
                last.then_inc(xp_ps, 1)
                for k in range(2):
                    last = mm(XT[0:H, k * 512:(k + 1) * 512], W1[:, D + H:D + 2 * H],
                              x1T[:, k * 512:(k + 1) * 512], start=True, stop=True)
                last.then_inc(es_ps, 1)

            def step(b, q, half):
                if not is_last(b):
                    front(b + 1, 1 - q, half + q)
                products(b, q)
                if not is_first(b):
                    proj(b - 1, BS if is_last(b) else b + 2)

            front(0, 0, 0)
            l0_steps(pe, step)
            proj(BS - 1, BS)

            pe.wait_ge(head_ok, 1)
            pe.wait_ge(es_ok, BS)
            pe.wait_ge(xp_ok, BS)
            pe.wait_ge(out_rd, BS)

            def head(b, h):
                n = b * H + h
                pe.wait_ge(hm_ok, n + 1)
                pe.wait_ge(V_ok, n + 1)
                if not (isinstance(b, int) and n < 2):
                    pe.wait_ge(red_ok, n - 1)
                hi = V[h % 4][:].bitcast(BF16).rearrange("p t f (k u) -> p t (f k) u", u=2)[:, :, :, 1]
                csn = csum3[:, bass.ds(n, 1), :, :].bitcast(BF16).rearrange("p o f (k u) -> p (o f k) u", u=2)[:, :, 1]
                W3 = VW * 3
                for t in range(NT):
                    o = acc[h % 2][:, t // 4, (t % 4) * W3:(t % 4 + 1) * W3]
                    od = o[:, W3 // 2:]
                    mm(o, emptyb[:, t * P:(t + 1) * P], csn, start=True, stop=False)
                    for c in range(NT):
                        mm(o, Hm[h % 2][:, c, t * P:(t + 1) * P], hi[:, c, :], start=False, stop=False)
                    for c in range(NT):
                        last = mm(od, GtN[:, c, t * P:(t + 1) * P], hi[:, c, W3 // 2:], start=False,
                                  stop=c == NT - 1)
                last.then_inc(hd_ps, 1)

            def transposes(b):
                pe.wait_ge(hc_ok, b + 1)
                for t in range(NT):
                    last = nc.tensor.transpose(TP[:, t * P:(t + 1) * P], hc[:, t, :], ident[:])
                last.then_inc(hT_ps, 1)

            def out_proj(b):
                pe.wait_ge(hT_ok, b + 1)
                if not is_first(b):
                    pe.wait_ge(op_rd, b)
                for t in range(NT):
                    last = mm(OPb[t // 4][:, (t % 4) * D:(t % 4 + 1) * D], hT[:, t * P:(t + 1) * P], WoT[:],
                              start=True, stop=True)
                last.then_inc(op_ps, 1)

            def l1_batch(b):
                for h in range(1, H):
                    head(b, h)
                    if not is_first(b):
                        if h == 1:
                            transposes(b - 1)
                        if h == 3:
                            out_proj(b - 1)
                if not is_last(b):
                    head(b + 1, 0)

            head(0, 0)
            l1_batch(0)
            with pe.Fori(1, BS - 1) as b:
                l1_batch(b)
            l1_batch(BS - 1)
            transposes(BS - 1)
            out_proj(BS - 1)


_INS = ['x', 'adj', 'L0_gnn_W', 'L0_gnn_a', 'L1_gnn_W', 'L1_gnn_a_src', 'L1_gnn_a_dst', 'L1_gnn_beta_tilde',
        'L1_gnn_W_out']


def kernel(**inputs):
    import numpy as _np
    import concourse.bacc as _bacc
    from concourse import mybir as _mybir
    from concourse.bass_utils import run_bass_kernel_spmd as _run

    nc = _bacc.Bacc("TRN2", target_bir_lowering=False, num_devices=1)
    arrays, args = {}, []
    for name in _INS:
        a = _np.ascontiguousarray(inputs[name])
        if a.ndim == 0:
            a = a.reshape(1)
        arrays[f"in_{name}_dram"] = a
        args.append(nc.dram_tensor(f"in_{name}_dram", a.shape, _mybir.dt.from_np(a.dtype), kind="ExternalInput").ap())
    out = nc.dram_tensor("out_0_dram", (BS, N, D), F32, kind="ExternalOutput").ap()
    gnn_kernel(nc, *args, out)
    r = _run(nc, [arrays], core_ids=[0])
    return r.results[0]["out_0_dram"]
```

```python
import concourse.bass as bass
from concourse import mybir
from contextlib import ExitStack

F32 = mybir.dt.float32
BF16 = mybir.dt.bfloat16
U8 = mybir.dt.uint8
FP8 = mybir.dt.float8e4
I32 = mybir.dt.int32
ALU = mybir.AluOpType
ACT = mybir.ActivationFunctionType
AX = mybir.AxisListType
RMAX = bass.bass_isa.ReduceOp.max

P = 128
BS, N, D, H = 8, 1024, 128, 8
NT = N // P
DH = D // H
NH = BS * H
KW = DH + 1
VW = 2 * KW
SLOPE = 0.2
LN_EPS = 1e-5
LOG_EPS = 1e-6
STEEP = 2.0 ** 60
EDGE_SHIFT = 5
EDGE_BYTE = 1 << EDGE_SHIFT
EDGE = 0.125
AC = (5, 7, 5, 5, 5, 7, 5, 6)
NC = 4


ACT_X1T, ACT_PROJ = 2, 5
DVE_NORM, DVE_PROJ = 2, 5
DVE_FINISH1, DVE_NORM1 = 5, 7
PE_X1T = 3


class Links:

    def __init__(self, eng, sem, per):
        self.eng, self.sem, self.per = eng, sem, per

    def begin(self, b):
        self.b, self.k = b, 0

    def link(self, ins):
        self.k += 1
        ins.then_inc(self.sem, 1)
        self.eng.wait_ge(self.sem, self.b * self.per + self.k)

    def end(self):
        assert self.k == self.per, (self.k, self.per)


def gnn_kernel(nc, x, adj, w0, a0, w1, a_src, a_dst, beta, w_out, out):
    ctx = ExitStack()
    with ctx:
        def sb(name, shape, dt=F32, where=ctx):
            return where.enter_context(nc.sbuf_tensor(name, shape, dt))

        def sem(name):
            return ctx.enter_context(nc.semaphore(name))

        x1_dram = nc.dram_tensor("x1_scratch", (BS, N, D), F32, kind="Internal").ap()
        es_dram = nc.dram_tensor("es_scratch", (NH, N), F32, kind="Internal").ap()

        ident = sb("ident", [P, P])
        identb = sb("identb", [P, P], BF16)
        ones_col = sb("ones_col", [P, 1], BF16)
        Gt = sb("Gt", [P, NT, N], FP8)
        GtN = sb("GtN", [P, NT, N], FP8)
        emptyb = sb("emptyb", [P, N], BF16)
        W0 = sb("W0", [P, D + 1])
        Wa1 = sb("Wa1", [P, P])
        W1 = sb("W1", [P, D + 2 * H])
        WoT = sb("WoT", [P, D])
        xp = sb("xp", [P, NT, BS * D])
        edes = sb("edes", [P, NT, 2, NH])
        csum3 = sb("csum3", [P, NH, VW, 3], BF16)
        csr = sb("csr", [1, D])
        crow0 = [sb(f"crow0{q}", [P, 3, D + 1], BF16) for q in range(2)]
        BD = sb("BD", [P, NT, NH, 2])
        R1 = sb("R1", [P, NT, NH])
        cmps = sb("cmps", [P, NH, 2, NT])
        cmph = [sb(f"cmph{q}", [P, 2, NT]) for q in range(4)]
        edp = sb("edp", [P, NT, NH])
        esm = sb("esm", [P, NT, NH])
        Dexp = sb("Dexp", [P, NT, NH])
        m64 = sb("m64", [P, NH])
        M64 = sb("M64", [P, NH])
        lp = sb("lp", [P, 1])
        tiny = sb("tiny", [P, 8])
        stats = sb("stats", [P, NT, 6])
        mv = sb("mv", [P, NT, 2])
        rstd = sb("rstd", [P, NT])
        rstd_e = sb("rstd_e", [P, NT])
        lneps = sb("lneps", [P, NT])
        mhalf = sb("mhalf", [P, NT])
        rden = sb("rden", [P, NT * H])
        rslope = sb("rslope", [P, 1])
        idle = sb("idle", [P, 1])
        idle_v = sb("idle_v", [P, 1])

        L0 = ExitStack()
        Pt = [sb(f"Pt{q}", [P, NT, N], F32, L0) for q in range(2)]
        xin = [sb(f"xin{q}", [P, NT, D], F32, L0) for q in range(2)]
        xres0 = [sb(f"xres0{q}", [P, NT, D], F32, L0) for q in range(2)]
        hA = [sb(f"hA{q}", [P, NT, D + 1], F32, L0) for q in range(2)]
        x1b = sb("x1b", [P, NT, D], F32, L0)
        xT = sb("xT", [P, N], F32, L0)
        Rb = sb("Rb", [P, N], F32, L0)
        hp = [sb(f"hp{q}", [P, NT, D], F32, L0) for q in range(2)]
        et = sb("et", [P, NT, D], F32, L0)
        es_row = sb("es_row", [H, N], F32, L0)
        csx = [sb(f"csx_{q}", [P, 1], F32, L0) for q in range(2)]
        csx1 = sb("csx_l1", [P, 1], F32, L0)
        s2c = sb("s2c", [P, NT], F32, L0)
        s2p = sb("s2p", [P, NT], F32, L0)
        smax = sb("smax", [P, 4], F32, L0)
        bd = [sb(f"bd{q}", [P, 3 * NT], F32, L0) for q in range(2)]
        adj_in = [Pt[1][:, s, :].bitcast(I32) for s in range(4)]
        Gi = [Pt[1][:, 4, s * 512:(s + 1) * 512].bitcast(BF16) for s in range(2)]
        wraw = Pt[1][:, 5, 0:P]
        woraw = Pt[1][:, 5, P:2 * P]
        asb = Pt[1][:, 5, 2 * P:3 * P]
        adb = Pt[1][:, 5, 3 * P:4 * P]
        wprod = Pt[1][:, 5, 4 * P:6 * P]
        w0T = Pt[1][:, 6, 0:P]
        a1c = Pt[1][:, 6, P:P + 2]
        a1r = Pt[1][:, 6, 2 * P:3 * P]
        L0.close()

        C = [sb(f"C{q}", [P, NT, N], U8) for q in range(2)]
        srow = [sb(f"srow{q}", [P, N]) for q in range(4)]
        Hm = [sb(f"Hm{q}", [P, NT, N], FP8) for q in range(2)]
        V = [sb(f"V{q}", [P, NT, VW, 3]) for q in range(4)]
        sb("pad", [P, (2 * N * NT - 4 * 3 * VW * NT * 4) // 4])
        C += [sb(f"C{q}", [P, NT, N], U8) for q in range(2, NC)]
        xres = sb("xres", [P, NT, D])
        hT = sb("hT", [P, N])
        Sb = sb("Sb", [P, NT, H, VW])
        hc = sb("hc", [P, NT, D])
        yout = sb("yout", [P, NT, D])

        XT = ctx.enter_context(nc.psum_tensor("XT", [P, 1024], F32))
        HH = ctx.enter_context(nc.psum_tensor("HH", [P, 3, 512], F32))
        OUT = ctx.enter_context(nc.psum_tensor("OUT", [P, 3, 512], F32))
        cs0_ps = HH[0:1, 2, 258:386]
        cs1_ps = HH[0:1, 2, 300:428]
        acc = [HH[:, 0:2, :], OUT[:, 0:2, :]]
        TP = XT
        OPb = [HH[:, 2, :], OUT[:, 2, :]]

        def third(t, w):
            return [(t[:, 0:2, 0:3 * w].rearrange("p k (t w) -> p k t w", w=w), 0, 6),
                    (t[:, 2, 0:2 * w].rearrange("p (t w) -> p t w", w=w), 6, 8)]

        adj_ld = [sem(f"adj_ld{s}") for s in range(4)]
        w_ld, const_ok = sem("w_ld"), sem("const_ok")
        gi_ok, gT_ps, gt_ok, gtn_ok = sem("gi_ok"), sem("gT_ps"), sem("gt_ok"), sem("gtn_ok")
        deg_ps, empty_ok = sem("deg_ps"), sem("empty_ok")
        wT_ps, wT_ok, wa_ps, w_ok = sem("wT_ps"), sem("wT_ok"), sem("wa_ps"), sem("w_ok")
        lp_lnk, set_lnk = sem("lp_lnk"), sem("set_lnk")
        xin_ld = [sem(f"xin_ld{q}") for q in range(2)]
        xr0_ld = [sem(f"xr0_ld{q}") for q in range(2)]
        xT_ps, xT_ok, h_ps, s1_ps = sem("xT_ps"), sem("xT_ok"), sem("h_ps"), sem("s1_ps")
        h_ok, mx_ok, gmx_ok, s2_ok, bd_lnk, R_ok = [sem(n) for n in
            ("h_ok", "mx_ok", "gmx_ok", "s2_ok", "bd_lnk", "R_ok")]
        relu_ok, P_ok, out_ps, out_rd, min_ok, elu_ok = [sem(n) for n in
            ("relu_ok", "P_ok", "out_ps", "out_rd", "min_ok", "elu_ok")]
        rs_ok, rs1_ok = sem("rs_ok"), sem("rs1_ok")
        mv_ok, x1_ok, x1_st, x1T_ps, x1T_ok = [sem(n) for n in
            ("mv_ok", "x1_ok", "x1_st", "x1T_ps", "x1T_ok")]
        xp_ps, xp_ok, ed_ok, es_ps, es_ok, es_st = [sem(n) for n in
            ("xp_ps", "xp_ok", "ed_ok", "es_ps", "es_ok", "es_st")]
        f_lnk, m_lnk, n_lnk, p_lnk, pf_lnk, pm_lnk = [sem(n) for n in
            ("f_lnk", "m_lnk", "n_lnk", "p_lnk", "pf_lnk", "pm_lnk")]
        pad_ok, cmp_ok = sem("pad_ok"), sem("cmp_ok")
        ed_mx, ed_gmx, edp_ok, bexp_ok, head_ok, z_lnk = [sem(n) for n in
            ("ed_mx", "ed_gmx", "edp_ok", "bexp_ok", "head_ok", "z_lnk")]
        srow_ld = [sem(f"srow_ld{q}") for q in range(4)]
        V_ok, v_lnk, ccmp_a, ccmp_v, hm_ok, hd_ps, red_ok = [sem(n) for n in
            ("V_ok", "v_lnk", "ccmp_a", "ccmp_v", "hm_ok", "hd_ps", "red_ok")]
        hc_ok, hT_ps, hT_ok, op_ps, op_rd, y_ok, y_st, xres_ld = [sem(n) for n in
            ("hc_ok", "hT_ps", "hT_ok", "op_ps", "op_rd", "y_ok", "y_st", "xres_ld")]
        k_lnk, t_lnk, mv1_ok, pt_lnk = [sem(n) for n in ("k_lnk", "t_lnk", "mv1_ok", "pt_lnk")]

        x_t = x.rearrange("b (t p) d -> b p t d", p=P)
        x1_t = x1_dram.rearrange("b (t p) d -> b p t d", p=P)
        out_t = out.rearrange("b (t p) d -> b p t d", p=P)
        adj_t = adj.rearrange("(t p) j -> t p j", p=P)
        N_W = 8

        def l0_steps(eng, body):
            body(0, 0, 0)
            body(1, 1, 0)
            with eng.Fori(0, (BS - 4) // 2) as t:
                body(t * 2 + 2, 0, t + 1)
                body(t * 2 + 3, 1, t + 1)
            body(BS - 2, 0, BS // 2 - 1)
            body(BS - 1, 1, BS // 2 - 1)

        def is_first(b):
            return isinstance(b, int) and b == 0

        def before(b, n):
            return isinstance(b, int) and b < n

        def is_last(b):
            return isinstance(b, int) and b == BS - 1

        block = ctx.enter_context(nc.Block())

        @block.sync
        def _(sp):
            sp.dma_start(wraw, w0).then_inc(w_ld, 16)
            sp.dma_start(W1[:, 0:D].rearrange("d (h f) -> d h f", h=H),
                         w1.rearrange("h d f -> d h f")).then_inc(w_ld, 16)
            for k in range(2):
                sp.dma_start(a1c[:, k:k + 1], a0[k * P:(k + 1) * P, :]).then_inc(w_ld, 16)
            sp.dma_start(asb, a_src.rearrange("h f -> (h f)").partition_broadcast(P)).then_inc(w_ld, 16)
            sp.dma_start(adb, a_dst.rearrange("h f -> (h f)").partition_broadcast(P)).then_inc(w_ld, 16)
            sp.dma_start(woraw, w_out).then_inc(w_ld, 16)
            sp.dma_start(lp[:], beta.partition_broadcast(P)).then_inc(w_ld, 16)
            sp.dma_start(xin[0][:], x_t[0]).then_inc(xin_ld[0], 16)
            for t in range(NT):
                if t >= 4:
                    sp.wait_ge(gi_ok, t - 3)
                sp.dma_start(adj_in[t % 4], adj_t[t]).then_inc(adj_ld[t % 4], 16)
            sp.dma_start(xin[1][:], x_t[1]).then_inc(xin_ld[1], 16)
            for q in range(2):
                sp.dma_start(xres0[q][:], x_t[q]).then_inc(xr0_ld[q], 16)

            def load_in(b, q):
                sp.wait_ge(xT_ps, b + 1)
                sp.dma_start(xin[q][:], x_t[bass.ds(b + 2, 1)].rearrange("o p t d -> (o p) t d")
                             if not isinstance(b, int) else x_t[b + 2]).then_inc(xin_ld[q], 16)

            def load_res(b, q):
                sp.dma_start(xres0[q][:], x_t[bass.ds(b + 2, 1)].rearrange("o p t d -> (o p) t d")
                             if not isinstance(b, int) else x_t[b + 2]).then_inc(xr0_ld[q], 16)

            def store_es(b):
                sp.wait_ge(es_ok, b + 1)
                sp.dma_start(es_dram[bass.ds(b * H, H), :], es_row[:]).then_inc(es_st, 16)

            def store_x1(b):
                sp.wait_ge(x1_ok, b + 1)
                sp.dma_start(x1_t[bass.ds(b, 1)].rearrange("o p t d -> (o p) t d")
                             if not isinstance(b, int) else x1_t[b], x1b[:]).then_inc(x1_st, 16)

            def step(b, q):
                if not (isinstance(b, int) and b >= BS - 2):
                    load_in(b, q)
                if not before(b, 2):
                    store_es(b - 2)
                if not is_first(b):
                    store_x1(b - 1)
                    if not is_last(b):
                        load_res(b - 1, 1 - q)

            step(0, 0)
            step(1, 1)
            with sp.Fori(0, (BS - 4) // 2) as t:
                step(t * 2 + 2, 0)
                step(t * 2 + 3, 1)
            step(BS - 2, 0)
            step(BS - 1, 1)
            sp.wait_ge(es_st, 16)
            sp.wait_ge(cmp_ok, 1)
            sp.wait_ge(out_ps, BS - 1)

            def load_row(b, h):
                n = b * H + h
                if not (isinstance(b, int) and n < 4):
                    sp.wait_ge(ccmp_a, n - 3)
                    sp.wait_ge(ccmp_v, n - 3)
                sp.dma_start(srow[h % 4][:], es_dram[bass.ds(n, 1), :].rearrange("o n -> (o n)")
                             .partition_broadcast(P)).then_inc(srow_ld[h % 4], 16)
                sp.dma_start(cmph[h % 4][:].rearrange("p k t -> p (k t)"),
                             cmps[:, bass.ds(n, 1), :, :].rearrange("p o k t -> p (o k t)")).then_inc(srow_ld[h % 4], 16)

            for h in range(4):
                load_row(0, h)
            store_es(6)
            store_x1(7)
            store_es(7)
            for h in range(4, H):
                load_row(0, h)
            sp.wait_ge(es_st, 16 * BS)
            with sp.Fori(1, BS) as b:
                for h in range(H):
                    load_row(b, h)

        @block.gpsimd
        def _(pool):
            pool.memset(ident[:], 0.0).then_inc(set_lnk, 1)
            pool.wait_ge(set_lnk, 1)
            pool.affine_select(out=ident[:], in_=ident[:], compare_op=ALU.not_equal, fill=1.0, base=0,
                               pattern=[[-1, P]], channel_multiplier=1).then_inc(set_lnk, 1)
            pool.wait_ge(set_lnk, 2)
            pool.tensor_copy(identb[:], ident[:])
            pool.memset(ones_col[:], 1.0)
            pool.memset(lneps[:], LN_EPS)
            pool.memset(mhalf[:], -0.5)
            pool.memset(rslope[:], 1.0 - SLOPE)
            pool.memset(tiny[:], 0.0).then_inc(const_ok, 1)
            for q in range(2):
                pool.memset(crow0[q][:], 0.0).then_inc(set_lnk, 1)
            pool.wait_ge(set_lnk, 4)
            for q in range(2):
                pool.memset(crow0[q][0:1, 0, D:D + 1], float(N))
                pool.memset(hA[q][:, :, D:D + 1], 1.0)
            pool.memset(emptyb[:], 0.0).then_inc(pad_ok, 1)

            pf = Links(pool, pf_lnk, 1)
            pm = Links(pool, pm_lnk, 1)

            def front(b):
                pf.begin(b)
                pool.wait_ge(mx_ok, b + 1)
                if not is_first(b):
                    pool.wait_ge(R_ok, b)
                pool.tensor_tensor(idle[:], lneps[:, 0:1], lneps[:, 0:1], ALU.add)
                pf.link(pool.partition_all_reduce(smax[:, 1:2], smax[:, 0:1], P, RMAX))
                pool.tensor_tensor(smax[:, 2:3], smax[:, 1:2], rslope[:], ALU.mult).then_inc(gmx_ok, 1)
                pf.end()

            def rsqrt(links, b, ready, done):
                links.begin(b)
                pool.wait_ge(ready, b + 1)
                links.link(pool.tensor_tensor(rstd_e[:], mv[:, :, 1], lneps[:], ALU.add))
                pool.tensor_tensor(rstd[:], rstd_e[:], mhalf[:], ALU.pow).then_inc(done, 1)
                links.end()

            front(0)
            pool.memset(csum3[:], 0.0).then_inc(set_lnk, 1)
            pool.wait_ge(set_lnk, 5)
            pool.memset(csum3[0:1, :, VW - 1, 0], float(N)).then_inc(pad_ok, 1)

            def step(b, q, _):
                if not is_last(b):
                    front(b + 1)
                if not is_first(b):
                    rsqrt(pm, b - 1, mv_ok, rs_ok)
            l0_steps(pool, step)
            rsqrt(pm, BS - 1, mv_ok, rs_ok)

            pool.wait_ge(ed_mx, 1)
            pool.partition_all_reduce(M64[:], m64[:], P, RMAX).then_inc(ed_gmx, 1)
            pool.wait_ge(head_ok, 1)

            vl = Links(pool, v_lnk, 2)

            def values(b, h):
                n = b * H + h
                vl.begin(n)
                if not (isinstance(b, int) and n < 4):
                    pool.wait_ge(hd_ps, n - 3)
                v = V[h % 4]
                bdn = BD[:, :, bass.ds(n, 1), :].rearrange("p t o k -> p t (o k)")
                f0 = bass.ds(b * D + h * DH, DH)
                vk = v[:, :, :, 0].rearrange("p t (k f) -> p t k f", k=2)
                for k in range(2):
                    pool.tensor_tensor(vk[:, :, k, 0:DH], xp[:, :, f0],
                                       bdn[:, :, k:k + 1].to_broadcast([P, NT, DH]), ALU.mult)
                vl.link(pool.tensor_copy(vk[:, :, :, DH:KW].rearrange("p t k o -> p t (k o)"), bdn))
                hi = v[:].bitcast(BF16).rearrange("p t f (k u) -> p (t f) k u", u=2)[:, :, :, 1]
                w = v[:].rearrange("p t f k -> p (t f) k")
                vl.link(pool.tensor_tensor(w[:, :, 1], w[:, :, 0], hi[:, :, 0], ALU.subtract))
                pool.tensor_tensor(w[:, :, 2], w[:, :, 1], hi[:, :, 1], ALU.subtract).then_inc(V_ok, 1)
                vl.end()

            pt = Links(pool, pt_lnk, 1)

            def l1_batch(b):
                for h in range(H):
                    values(b, h)
                    if h == H - 1 and not is_first(b):
                        rsqrt(pt, b - 1, mv1_ok, rs1_ok)
            l1_batch(0)
            with pool.Fori(1, BS) as b:
                l1_batch(b)
            rsqrt(pt, BS - 1, mv1_ok, rs1_ok)

        @block.scalar
        def _(act):
            a = nc.scalar
            act.wait_ge(w_ld, 16 * N_W)
            act.wait_ge(const_ok, 1)

            def chain(ins, k):
                ins.then_inc(lp_lnk, 1)
                act.wait_ge(lp_lnk, k)
            chain(a.activation(tiny[:, 0:1], lp[:], ACT.Abs), 1)
            chain(a.activation(tiny[:, 1:2], tiny[:, 0:1], ACT.Exp, scale=-1.0), 2)
            chain(a.activation(tiny[:, 2:3], tiny[:, 1:2], ACT.Ln, bias=1.0), 3)
            chain(a.activation(tiny[:, 3:4], lp[:], ACT.Relu, bias=0.0), 4)
            chain(a.activation(tiny[:, 5:6], tiny[:, 4:5], ACT.Ln, bias=1.0 + LOG_EPS), 5)

            def negate_mask(t0, t1):
                a.activation(GtN[:, t0:t1, :], Gt[:, t0:t1, :], ACT.Copy, scale=-1.0, saturate=False)\
                 .then_inc(gtn_ok, 1)

            bdl = Links(act, bd_lnk, 3)

            def copy_xT(b, q):
                act.wait_ge(xT_ps, b + 1)
                a.activation(xT[:], XT[:], ACT.Copy, accum_out=csx[q][:]).then_inc(xT_ok, 1)

            def front(b, q):
                act.wait_ge(mx_ok, b + 1)
                for v, t0, t1 in third(HH, D + 1):
                    last = a.activation(hA[q][:, t0:t1, 0:D] if t0 else
                                        hA[q][:, t0:t1, 0:D].rearrange("p (k t) d -> p k t d", k=2),
                                        v[..., 0:D], ACT.Copy)
                last.then_inc(h_ok, 1)
                if not before(b, 2):
                    elu(b - 2)
                act.wait_ge(s2_ok, b + 1)
                bdl.begin(b)
                bdl.link(a.activation(bd[q][:, 0:NT], s2p[:], ACT.Exp))
                bdl.link(a.activation(bd[q][:, NT:2 * NT], s2p[:], ACT.Exp, scale=SLOPE))
                bdl.link(a.activation(bd[q][:, 2 * NT:], bd[q][:, NT:2 * NT], ACT.Copy, scale=-1.0))
                bdl.end()
                act.wait_ge(s1_ps, b + 1)
                act.wait_ge(gmx_ok, b + 1)
                a.activation(Rb[:], XT[:], ACT.Exp, scale=1.0 - SLOPE, bias=smax[:, 2:3]).then_inc(R_ok, 1)

            def scores(b, q, between):
                act.wait_ge(R_ok, b + 1)
                if not (isinstance(b, int) and b < 2):
                    act.wait_ge(out_ps, b - 1)
                for c in range(NT):
                    a.activation(Pt[q][:, c, :], Rb[:], ACT.Relu, scale=bd[q][:, c:c + 1],
                                 bias=bd[q][:, 2 * NT + c:2 * NT + c + 1]).then_inc(relu_ok, 1)
                    if between and c in between:
                        between[c]()

            def copy_x1T(b):
                act.wait_ge(x1T_ps, b + 1)
                a.activation(xT[:], XT[:], ACT.Copy, accum_out=csx1[:]).then_inc(x1T_ok, 1)

            def copy_proj(b):
                act.wait_ge(ed_ok, b + 1)
                for v, t0, t1 in third(HH, D + 2 * H):
                    o = xp[:, t0:t1, bass.ds(b * D, D)]
                    last = a.activation(o if t0 else o.rearrange("p (k t) d -> p k t d", k=2),
                                        v[..., 0:D], ACT.Copy)
                last.then_inc(xp_ok, 1)
                act.wait_ge(es_ps, b + 1)
                if not is_first(b):
                    act.wait_ge(es_st, b * 16)
                a.activation(es_row[:], XT[0:H, :], ACT.Copy).then_inc(es_ok, 1)

            def elu(b):
                act.wait_ge(min_ok, b + 1)
                a.activation(et[:], et[:], ACT.Exp).then_inc(elu_ok, 1)

            def step(b, q, _):
                if not is_last(b):
                    front(b + 1, 1 - q)
                between = {}
                if not before(b, 2):
                    between[ACT_X1T] = lambda: copy_x1T(b - 2)
                    between[ACT_PROJ] = lambda: copy_proj(b - 2)
                if is_last(b):
                    elu(b - 1)
                    for c in sorted(between):
                        between[c]()
                else:
                    scores(b + 1, 1 - q, between)
                if not (isinstance(b, int) and b >= BS - 2):
                    copy_xT(b + 2, q)

            copy_xT(0, 0)
            front(0, 0)
            scores(0, 0, None)
            copy_xT(1, 1)
            act.wait_ge(gt_ok, NT)
            act.wait_ge(w_ok, 1)
            act.wait_ge(gT_ps, NT)
            l0_steps(act, step)

            def compare(b, h):
                n = b * H + h
                act.wait_ge(srow_ld[h % 4], (b * 2 + h // 4 + 1) * 32)
                if not (isinstance(b, int) and n < NC):
                    act.wait_ge(hm_ok, n - NC + 1)
                for c in range(AC[h]):
                    last = a.activation(C[h % NC][:, c, :], srow[h % 4][:], ACT.Sigmoid, scale=STEEP,
                                        bias=cmph[h % 4][:, 0, c:c + 1])
                last.then_inc(ccmp_a, 1)

            for k in range(2):
                compare(0, k)
                negate_mask(k * 4, k * 4 + 4)
            copy_x1T(BS - 2)
            copy_proj(BS - 2)
            elu(BS - 1)
            copy_x1T(BS - 1)
            copy_proj(BS - 1)

            act.wait_ge(edp_ok, 1)
            a.activation(BD[:, :, :, 0], edp[:], ACT.Exp, bias=lp[:])
            a.activation(Dexp[:], edp[:], ACT.Exp, scale=SLOPE, bias=lp[:])
            a.activation(R1[:], esm[:], ACT.Exp, scale=1.0 - SLOPE).then_inc(bexp_ok, 1)
            def copy_hT(b):
                act.wait_ge(hT_ps, b + 1)
                a.activation(hT[:], TP[:], ACT.Copy).then_inc(hT_ok, 1)

            def store_y(b):
                act.wait_ge(y_ok, b + 1)
                act.dma_start(out_t[b] if isinstance(b, int) else
                              out_t[bass.ds(b, 1)].rearrange("o p t d -> (o p) t d"), yout[:]).then_inc(y_st, 16)

            def load_res(b):
                act.dma_start(xres[:], x1_t[b] if isinstance(b, int) else
                              x1_t[bass.ds(b, 1)].rearrange("o p t d -> (o p) t d")).then_inc(xres_ld, 16)

            def l1_batch(b):
                for h in range(2 if is_first(b) else 0, H):
                    compare(b, h)
                    if h == 3 and not is_first(b):
                        if not before(b, 2):
                            store_y(b - 2)
                        load_res(b - 1)
                    if h == 5 and not is_first(b):
                        copy_hT(b - 1)
            l1_batch(0)
            act.wait_ge(x1_st, 16 * BS)
            l1_batch(1)
            with act.Fori(2, BS) as b:
                l1_batch(b)
            store_y(BS - 2)
            load_res(BS - 1)
            copy_hT(BS - 1)
            store_y(BS - 1)
            act.wait_ge(y_st, 16 * BS)

        @block.vector
        def _(dve):
            v = nc.vector
            dve.wait_ge(const_ok, 1)
            dve.wait_ge(w_ld, 16 * N_W)
            for k, (vec, col) in enumerate(((adb, D), (asb, D + H))):
                v.tensor_tensor(wprod[:, k * D:(k + 1) * D], W1[:, 0:D], vec, ALU.mult)
            v.tensor_copy(a1r, a1c[:, 0:1].to_broadcast([P, P])).then_inc(z_lnk, 1)
            dve.wait_ge(z_lnk, 1)
            v.tensor_reduce(W1[:, D:D + 2 * H], wprod.rearrange("p (h f) -> p h f", f=DH), AX.X, ALU.add)
            dve.wait_ge(wT_ps, 1)
            v.tensor_copy(w0T, XT[:, 0:P])
            v.tensor_copy(WoT[:], XT[:, P:2 * P])
            v.tensor_copy(W0[:, 0:D], wraw).then_inc(wT_ok, 1)
            dve.wait_ge(wa_ps, 1)
            v.tensor_copy(Wa1[:], XT[:, 2 * P:3 * P])
            v.tensor_copy(W0[:, D:D + 1], XT[:, 3 * P:3 * P + 1]).then_inc(z_lnk, 1)
            dve.wait_ge(lp_lnk, 5)
            v.tensor_tensor(tiny[:, 6:7], tiny[:, 2:3], tiny[:, 3:4], ALU.add).then_inc(z_lnk, 1)
            dve.wait_ge(z_lnk, 3)
            v.tensor_tensor(lp[:], tiny[:, 6:7], tiny[:, 5:6], ALU.mult).then_inc(w_ok, 1)
            def mask_copy(t):
                dve.wait_ge(gT_ps, t + 1)
                v.tensor_copy(Gt[:, :, t * P:(t + 1) * P],
                              OUT[:, t % 2, :].bitcast(BF16).rearrange("p (c i) -> p c i", c=NT), saturate=False).then_inc(gt_ok, 1)

            def mask_all():
                for t in range(NT):
                    dve.wait_ge(adj_ld[t % 4], 16 * (t // 4 + 1))
                    if t >= 2:
                        dve.wait_ge(gT_ps, t - 1)
                    v.tensor_scalar(Gi[t % 2], adj_in[t % 4], 0, EDGE, ALU.is_gt, ALU.mult).then_inc(gi_ok, 1)
                    if t >= 1:
                        mask_copy(t - 1)
                mask_copy(NT - 1)

            def empty_rows():
                dve.wait_ge(deg_ps, 1)
                dve.wait_ge(pad_ok, 1)
                v.tensor_scalar(emptyb[0:1, :], XT[0:1, :], 0.0, EDGE, ALU.is_equal, ALU.mult).then_inc(empty_ok, 1)

            def three_parts(links, src, rest, hi, mid, lo):
                links.link(v.tensor_copy(hi, src))
                links.link(v.tensor_tensor(rest, src, hi, ALU.subtract))
                links.link(v.tensor_copy(mid, rest))
                return v.tensor_tensor(lo, rest, mid, ALU.subtract)

            fl = Links(dve, f_lnk, 4)
            pl = Links(dve, p_lnk, 3)
            ml = Links(dve, m_lnk, 1)
            nl = Links(dve, n_lnk, 3)

            def front(b, q):
                fl.begin(b)
                dve.wait_ge(h_ps, b + 1)
                if not is_first(b):
                    dve.wait_ge(gmx_ok, b)
                for hv, t0, t1 in third(HH, D + 1):
                    s = s2c[:, t0:t1]
                    last = v.tensor_copy(s if t0 else s.rearrange("p (k t) -> p k t", k=2), hv[..., D])
                if not (isinstance(b, int) and b < 2):
                    dve.wait_ge(out_ps, b - 1)
                else:
                    dve.wait_ge(pad_ok, 1)
                cr = crow0[q][0:1, :, 0:D]
                fl.link(three_parts(fl, cs0_ps, csr[:], cr[:, 0], cr[:, 1], cr[:, 2]))
                v.tensor_reduce(smax[:, 0:1], s2c[:], AX.X, ALU.max).then_inc(mx_ok, 1)
                dve.wait_ge(gmx_ok, b + 1)
                if not is_first(b):
                    dve.wait_ge(R_ok, b)
                v.tensor_scalar(s2p[:], s2c[:], smax[:, 1:2], None, ALU.subtract).then_inc(s2_ok, 1)
                fl.end()

            def scores(b, q, between):
                for c in range(NT):
                    if between and c in between:
                        between[c]()
                    dve.wait_ge(relu_ok, b * NT + c + 1)
                    v.scalar_tensor_tensor(Pt[q][:, c, :], Pt[q][:, c, :], bd[q][:, NT + c:NT + c + 1],
                                           Gt[:, c, :].bitcast(U8), ALU.add, ALU.mult).then_inc(P_ok, 1)

            def layernorm_stats(links, y, done):
                for t in range(NT):
                    last = v.bn_stats(stats[:, t, :], y[:, t, :])
                links.link(last)
                v.tensor_copy(idle_v[:], lneps[:, 0:1])
                for t in range(NT):
                    last = v.bn_aggr(mv[:, t, :], stats[:, t, :])
                last.then_inc(done, 1)

            def divide(b, q):
                ml.begin(b)
                dve.wait_ge(out_ps, b + 1)
                for o, t0, t1 in third(OUT, D + 1):
                    r = rden[:, t0:t1]
                    last = v.reciprocal(r if t0 else r.rearrange("p (k t) -> p k t", k=2), o[..., D])
                ml.link(last)
                for o, t0, t1 in third(OUT, D + 1):
                    if t0:
                        last = v.tensor_tensor(hp[q][:, t0:t1, :], o[..., 0:D],
                                               rden[:, t0:t1].unsqueeze(2).to_broadcast([P, t1 - t0, D]), ALU.mult)
                    else:
                        v.tensor_tensor(hp[q][:, 0:6, :].rearrange("p (k t) d -> p k t d", k=2), o[..., 0:D],
                                        rden[:, 0:6].rearrange("p (k t) -> p k t", k=2).unsqueeze(3)
                                        .to_broadcast([P, 2, 3, D]), ALU.mult)
                last.then_inc(out_rd, 1)
                dve.wait_ge(out_rd, b + 1)
                if not is_first(b):
                    dve.wait_ge(n_lnk, b * 3)
                v.tensor_scalar(et[:], hp[q][:], 0.0, None, ALU.min).then_inc(min_ok, 1)
                ml.end()

            def finish(b, q, half):
                nl.begin(b)
                dve.wait_ge(xr0_ld[q], (half + 1) * 16)
                nl.link(v.scalar_tensor_tensor(hp[q][:], hp[q][:], 0.0, xres0[q][:], ALU.max, ALU.add))
                dve.wait_ge(elu_ok, b + 1)
                nl.link(v.scalar_tensor_tensor(hp[q][:], et[:], -1.0, hp[q][:], ALU.add, ALU.add))
                layernorm_stats(nl, hp[q], mv_ok)
                nl.end()

            def layernorm_scale(dst, y):
                for t in range(NT):
                    last = v.tensor_scalar(dst[:, t, :], y[:, t, :], mv[:, t, 0:1], rstd[:, t:t + 1],
                                           ALU.subtract, ALU.mult)
                return last

            def normalise(b, q):
                dve.wait_ge(rs_ok, b + 1)
                if not is_first(b):
                    dve.wait_ge(x1_st, b * 16)
                    dve.wait_ge(x1T_ps, b)
                layernorm_scale(x1b, hp[q]).then_inc(x1_ok, 1)

            def proj(b):
                pl.begin(b)
                dve.wait_ge(xp_ps, b + 1)
                for hv, t0, t1 in third(HH, D + 2 * H):
                    for k in range(2):
                        o = edes[:, t0:t1, k, bass.ds(b * H, H)]
                        v.tensor_copy(o if t0 else o.rearrange("p (k t) h -> p k t h", k=2),
                                      hv[..., D + k * H:D + (k + 1) * H])
                if is_first(b):
                    dve.wait_ge(pad_ok, 2)
                c3 = [csum3[0:1, bass.ds(b * H, H), KW:VW - 1, k] for k in range(3)]
                three_parts(pl, cs1_ps.rearrange("o (h f) -> o h f", h=H),
                            csr[:].rearrange("o (h f) -> o h f", h=H), *c3).then_inc(ed_ok, 1)
                edn = edes[:, :, 0, bass.ds(b * H, H)].rearrange("p t e -> p e t")
                v.tensor_scalar(cmps[:, bass.ds(b * H, H), 0, :], edn, STEEP, None, ALU.mult)
                v.tensor_scalar(cmps[:, bass.ds(b * H, H), 1, :], edn, -1.0, None, ALU.mult).then_inc(cmp_ok, 1)
                pl.end()

            def step(b, q, half):
                if not is_last(b):
                    front(b + 1, 1 - q)
                if not is_first(b):
                    finish(b - 1, 1 - q, half + q - 1)
                between = {}
                if not before(b, 2):
                    between[DVE_PROJ] = lambda: proj(b - 2)
                if not is_first(b):
                    between[DVE_NORM] = lambda: normalise(b - 1, 1 - q)
                if is_last(b):
                    for c in sorted(between, reverse=True):
                        between[c]()
                    compare(0, 0)
                    compare(0, 1)
                else:
                    scores(b + 1, 1 - q, between)
                divide(b, q)

            def compare(b, h):
                n = b * H + h
                dve.wait_ge(srow_ld[h % 4], (b * 2 + h // 4 + 1) * 32)
                if not (isinstance(b, int) and n < NC):
                    dve.wait_ge(hm_ok, n - NC + 1)
                for c in range(AC[h], NT):
                    last = v.tensor_scalar(C[h % NC][:, c, :], srow[h % 4][:], cmph[h % 4][:, 1, c:c + 1], None,
                                           ALU.is_gt)
                last.then_inc(ccmp_v, 1)

            front(0, 0)
            mask_all()
            dve.wait_ge(gt_ok, NT)
            scores(0, 0, {4: empty_rows})
            l0_steps(dve, step)
            proj(BS - 2)
            finish(BS - 1, 1, BS // 2 - 1)
            normalise(BS - 1, 1)
            proj(BS - 1)

            dve.wait_ge(cmp_ok, BS)
            v.tensor_reduce(m64[:], edes[:, :, 0, :].rearrange("p t e -> p e t"), AX.X, ALU.max).then_inc(ed_mx, 1)
            dve.wait_ge(ed_gmx, 1)
            mb = M64[:].unsqueeze(1).to_broadcast([P, NT, NH])
            v.tensor_tensor(edp[:], edes[:, :, 0, :], mb, ALU.subtract)
            v.tensor_tensor(esm[:], edes[:, :, 1, :], mb, ALU.add).then_inc(edp_ok, 1)
            dve.wait_ge(bexp_ok, 1)
            dve.wait_ge(out_ps, BS)
            v.tensor_scalar(BD[:, :, :, 1], Dexp[:], -1.0, None, ALU.mult).then_inc(head_ok, 1)

            kl = Links(dve, k_lnk, 3)
            tl = Links(dve, t_lnk, 1)

            def mask(b, h):
                n = b * H + h
                dve.wait_ge(ccmp_a, n + 1)
                dve.wait_ge(ccmp_v, n + 1)
                if not (isinstance(b, int) and n < 2):
                    dve.wait_ge(hd_ps, n - 1)
                v.scalar_tensor_tensor(Hm[h % 2][:].rearrange("p t n -> p (t n)").bitcast(I32),
                                       C[h % NC][:].rearrange("p t n -> p (t n)").bitcast(I32), EDGE_SHIFT,
                                       Gt[:].rearrange("p t n -> p (t n)").bitcast(I32),
                                       ALU.logical_shift_left, ALU.bitwise_and).then_inc(hm_ok, 1)

            def parts(b, h):
                n = b * H + h
                dve.wait_ge(hd_ps, n + 1)
                if h == 0 and not is_first(b):
                    dve.wait_ge(hc_ok, b)
                v.tensor_reduce(Sb[:, :, h, :].rearrange("p (k t) c -> p k t c", k=2),
                                acc[h % 2][:, :, 0:4 * VW * 3].rearrange("p k (t c s) -> p k t c s", s=3, c=VW),
                                AX.X, ALU.add).then_inc(red_ok, 1)

            def combine(b):
                kl.begin(b)
                dve.wait_ge(red_ok, (b + 1) * H)
                if not is_first(b):
                    dve.wait_ge(hT_ps, b)
                r = R1[:, :, bass.ds(b * H, H)].unsqueeze(3).to_broadcast([P, NT, H, KW])
                kl.link(v.tensor_tensor(Sb[:, :, :, 0:KW], Sb[:, :, :, 0:KW], r, ALU.mult))
                kl.link(v.tensor_tensor(Sb[:, :, :, 0:KW], Sb[:, :, :, 0:KW], Sb[:, :, :, KW:VW], ALU.add))
                kl.link(v.reciprocal(rden[:].rearrange("p (t h) -> p t h", h=H), Sb[:, :, :, DH]))
                v.tensor_tensor(hc[:].rearrange("p t (h f) -> p t h f", h=H), Sb[:, :, :, 0:DH],
                                rden[:].rearrange("p (t h) -> p t h", h=H).unsqueeze(3)
                                .to_broadcast([P, NT, H, DH]), ALU.mult).then_inc(hc_ok, 1)
                kl.end()

            def finish1(b):
                tl.begin(b)
                dve.wait_ge(op_ps, b + 1)
                dve.wait_ge(xres_ld, (b + 1) * 16)
                if not is_first(b):
                    dve.wait_ge(y_st, b * 16)
                for k in range(2):
                    last = v.tensor_tensor(yout[:, 4 * k:4 * k + 4, :], OPb[k].rearrange("p (t d) -> p t d", d=D),
                                           xres[:, 4 * k:4 * k + 4, :], ALU.add)
                last.then_inc(op_rd, 1)
                dve.wait_ge(op_rd, b + 1)
                layernorm_stats(tl, yout, mv1_ok)
                tl.end()

            def normalise1(b):
                dve.wait_ge(rs1_ok, b + 1)
                layernorm_scale(yout, yout).then_inc(y_ok, 1)

            def l1_batch(b):
                for h in range(1, H + 1):
                    if is_last(b) and h == H:
                        break
                    bb, hh = (b, h) if h < H else (b + 1, 0)
                    if not (is_last(b) and h == H - 1):
                        compare(*((bb, hh + 1) if hh + 1 < H else (b + 1, 0)))
                    if h >= 2:
                        parts(b, h - 2)
                    elif not is_first(b):
                        parts(b - 1, H - 1)
                    mask(bb, hh)
                    if not is_first(b):
                        if h == 1:
                            combine(b - 1)
                        if h == DVE_FINISH1:
                            finish1(b - 1)
                        if h == DVE_NORM1:
                            normalise1(b - 1)

            mask(0, 0)
            dve.wait_ge(x1_st, 16 * BS)
            l1_batch(0)
            with dve.Fori(1, BS - 1) as b:
                l1_batch(b)
            l1_batch(BS - 1)
            parts(BS - 1, H - 2)
            parts(BS - 1, H - 1)
            combine(BS - 1)
            finish1(BS - 1)
            normalise1(BS - 1)

        @block.tensor
        def _(pe):
            mm = nc.tensor.matmul
            pe.wait_ge(const_ok, 1)
            pe.wait_ge(w_ld, 16 * N_W)
            nc.tensor.transpose(XT[:, 0:P], wraw, ident[:])
            nc.tensor.transpose(XT[:, P:2 * P], woraw, ident[:]).then_inc(wT_ps, 1)
            pe.wait_ge(wT_ok, 1)
            mm(XT[:, 2 * P:3 * P], w0T, a1r, start=True, stop=True)
            mm(XT[:, 3 * P:3 * P + 1], w0T, a1c[:, 1:2], start=True, stop=True).then_inc(wa_ps, 1)
            def tile(t, ps, w):
                return ps[:, t // 3, (t % 3) * w:(t % 3 + 1) * w]

            def transpose_x(b, q, half):
                pe.wait_ge(xin_ld[q], (half + 1) * 16)
                if not before(b, 4):
                    pe.wait_ge(es_ok, b - 3)
                if not is_first(b):
                    pe.wait_ge(R_ok, b)
                for t in range(NT):
                    last = nc.tensor.transpose(XT[:, t * P:(t + 1) * P], xin[q][:, t, :], ident[:])
                last.then_inc(xT_ps, 1)

            def front(b, q):
                pe.wait_ge(xT_ok, b + 1)
                if not is_first(b):
                    pe.wait_ge(h_ok, b)
                if not before(b, 4):
                    pe.wait_ge(xp_ok, b - 3)
                mm(cs0_ps, csx[q][:], W0[:, 0:D], start=True, stop=True)
                for t in range(NT):
                    last = mm(tile(t, HH, D + 1), xT[:, t * P:(t + 1) * P], W0[:], start=True, stop=True)
                last.then_inc(h_ps, 1)
                for k in range(2):
                    last = mm(XT[:, k * 512:(k + 1) * 512], Wa1[:], xT[:, k * 512:(k + 1) * 512],
                              start=True, stop=True)
                last.then_inc(s1_ps, 1)

            def products(b, q, t0, t1):
                if t0 == 0:
                    pe.wait_ge(P_ok, (b + 1) * NT)
                    pe.wait_ge(h_ok, b + 1)
                    if not is_first(b):
                        pe.wait_ge(out_rd, b)
                for t in range(t0, t1):
                    o = tile(t, OUT, D + 1)
                    for c in range(NT):
                        mm(o, Pt[q][:, c, t * P:(t + 1) * P], hA[q][:, c, :], start=c == 0, stop=False)
                    for k in range(3):
                        last = mm(o, emptyb[:, t * P:(t + 1) * P], crow0[q][:, k, :], start=False, stop=k == 2)
                if t1 == NT:
                    last.then_inc(out_ps, 1)

            def transpose_x1(b, fronts):
                pe.wait_ge(x1_ok, b + 1)
                pe.wait_ge(R_ok, fronts)
                pe.wait_ge(h_ok, fronts)
                if not is_first(b):
                    pe.wait_ge(es_ok, b)
                    pe.wait_ge(xp_ok, b)
                for t in range(NT):
                    last = nc.tensor.transpose(XT[:, t * P:(t + 1) * P], x1b[:, t, :], ident[:])
                last.then_inc(x1T_ps, 1)

            def proj(b):
                pe.wait_ge(x1T_ok, b + 1)
                mm(cs1_ps, csx1[:], W1[:, 0:D], start=True, stop=True)
                for t in range(NT):
                    last = mm(tile(t, HH, D + 2 * H), xT[:, t * P:(t + 1) * P], W1[:], start=True, stop=True)
                last.then_inc(xp_ps, 1)
                for k in range(2):
                    last = mm(XT[0:H, k * 512:(k + 1) * 512], W1[:, D + H:D + 2 * H],
                              xT[:, k * 512:(k + 1) * 512], start=True, stop=True)
                last.then_inc(es_ps, 1)

            def step(b, q, half):
                if not is_last(b):
                    front(b + 1, 1 - q)
                products(b, q, 0, PE_X1T)
                if not before(b, 2):
                    transpose_x1(b - 2, BS if is_last(b) else b + 2)
                products(b, q, PE_X1T, PE_X1T + 1)
                if not before(b, 2):
                    proj(b - 2)
                products(b, q, PE_X1T + 1, NT - 1)
                if not (isinstance(b, int) and b >= BS - 2):
                    transpose_x(b + 2, q, half + 1)
                products(b, q, NT - 1, NT)

            pe.wait_ge(w_ok, 1)
            transpose_x(0, 0, 0)
            front(0, 0)
            for t in range(NT):
                pe.wait_ge(gi_ok, t + 1)
                if t >= 2:
                    pe.wait_ge(gt_ok, t - 1)
                for c in range(NT):
                    last = nc.tensor.transpose(OUT[:, t % 2, :].bitcast(BF16)[:, c * P:(c + 1) * P],
                                               Gi[t % 2][:, c * P:(c + 1) * P], identb[:])
                last.then_inc(gT_ps, 1)
            pe.wait_ge(gt_ok, NT)
            pe.wait_ge(R_ok, 1)
            for k in range(2):
                for c in range(NT):
                    last = mm(XT[0:1, k * 512:(k + 1) * 512], ones_col[:], Gt[:, c, k * 512:(k + 1) * 512],
                              start=c == 0, stop=c == NT - 1)
            last.then_inc(deg_ps, 1)
            pe.wait_ge(empty_ok, 1)
            transpose_x(1, 1, 0)
            l0_steps(pe, step)
            for b in (BS - 2, BS - 1):
                transpose_x1(b, BS)
                proj(b)

            pe.wait_ge(head_ok, 1)
            pe.wait_ge(es_ok, BS)
            pe.wait_ge(xp_ok, BS)
            pe.wait_ge(out_rd, BS)
            pe.wait_ge(gtn_ok, 2)

            def head(b, h):
                n = b * H + h
                pe.wait_ge(hm_ok, n + 1)
                pe.wait_ge(V_ok, n + 1)
                if not (isinstance(b, int) and n < 2):
                    pe.wait_ge(red_ok, n - 1)
                hi = V[h % 4][:].bitcast(BF16).rearrange("p t f (k u) -> p t (f k) u", u=2)[:, :, :, 1]
                csn = csum3[:, bass.ds(n, 1), :, :].rearrange("p o f k -> p (o f k)")
                W3 = VW * 3
                for t in range(NT):
                    o = acc[h % 2][:, t // 4, (t % 4) * W3:(t % 4 + 1) * W3]
                    od = o[:, W3 // 2:]
                    mm(o, emptyb[:, t * P:(t + 1) * P], csn, start=True, stop=False)
                    for c in range(NT):
                        mm(o, Hm[h % 2][:, c, t * P:(t + 1) * P], hi[:, c, :], start=False, stop=False)
                    for c in range(NT):
                        last = mm(od, GtN[:, c, t * P:(t + 1) * P], hi[:, c, W3 // 2:], start=False,
                                  stop=c == NT - 1)
                last.then_inc(hd_ps, 1)

            def transposes(b):
                pe.wait_ge(hc_ok, b + 1)
                for t in range(NT):
                    last = nc.tensor.transpose(TP[:, t * P:(t + 1) * P], hc[:, t, :], ident[:])
                last.then_inc(hT_ps, 1)

            def out_proj(b):
                pe.wait_ge(hT_ok, b + 1)
                if not is_first(b):
                    pe.wait_ge(op_rd, b)
                for t in range(NT):
                    last = mm(OPb[t // 4][:, (t % 4) * D:(t % 4 + 1) * D], hT[:, t * P:(t + 1) * P], WoT[:],
                              start=True, stop=True)
                last.then_inc(op_ps, 1)

            def l1_batch(b):
                for h in range(1, H):
                    head(b, h)
                    if not is_first(b):
                        if h == 1:
                            transposes(b - 1)
                        if h == 3:

                            out_proj(b - 1)
                if not is_last(b):
                    head(b + 1, 0)

            head(0, 0)
            l1_batch(0)
            with pe.Fori(1, BS - 1) as b:
                l1_batch(b)
            l1_batch(BS - 1)
            transposes(BS - 1)
            out_proj(BS - 1)


_INS = ['x', 'adj', 'L0_gnn_W', 'L0_gnn_a', 'L1_gnn_W', 'L1_gnn_a_src', 'L1_gnn_a_dst', 'L1_gnn_beta_tilde',
        'L1_gnn_W_out']


def kernel(**inputs):
    import numpy as _np
    import concourse.bacc as _bacc
    from concourse import mybir as _mybir
    from concourse.bass_utils import run_bass_kernel_spmd as _run

    nc = _bacc.Bacc("TRN2", target_bir_lowering=False, num_devices=1)
    arrays, args = {}, []
    for name in _INS:
        a = _np.ascontiguousarray(inputs[name])
        if a.ndim == 0:
            a = a.reshape(1)
        arrays[f"in_{name}_dram"] = a
        args.append(nc.dram_tensor(f"in_{name}_dram", a.shape, _mybir.dt.from_np(a.dtype), kind="ExternalInput").ap())
    out = nc.dram_tensor("out_0_dram", (BS, N, D), F32, kind="ExternalOutput").ap()
    gnn_kernel(nc, *args, out)
    r = _run(nc, [arrays], core_ids=[0])
    return r.results[0]["out_0_dram"]
```

```python
import concourse.bass as bass
from concourse import mybir
from contextlib import ExitStack

F32 = mybir.dt.float32
BF16 = mybir.dt.bfloat16
U8 = mybir.dt.uint8
FP8 = mybir.dt.float8e4
I32 = mybir.dt.int32
ALU = mybir.AluOpType
ACT = mybir.ActivationFunctionType
AX = mybir.AxisListType
RMAX = bass.bass_isa.ReduceOp.max

P = 128
BS, N, D, H = 8, 1024, 128, 8
NT = N // P
DH = D // H
NH = BS * H
KW = DH + 1
VW = 2 * KW
SLOPE = 0.2
LN_EPS = 1e-5
LOG_EPS = 1e-6
CAP = 80.0
STEEP = 2.0 ** 60
EDGE_SHIFT = 5
EDGE = 0.125
AC = (5, 6, 5, 7, 5, 6, 5, 7)
AC0 = (5, 6, 4, 5, 4, 5, 4, 4)
ACL = AC[:2] + (6, 7, 6, 7, 6, 7)
NC = 4

ACT_X1T, ACT_PROJ = 2, 5
DVE_PROJ = 5
T_FINISH, T_X1T, T_PROJ = 2, 3, 4
DVE_FINISH1, DVE_NORM1 = 5, 7
PE_LAST = 5
PE_X1T = 3


class Links:

    def __init__(self, eng, sem, per):
        self.eng, self.sem, self.per = eng, sem, per

    def begin(self, b):
        self.b, self.k = b, 0

    def link(self, ins):
        self.k += 1
        ins.then_inc(self.sem, 1)
        self.eng.wait_ge(self.sem, self.b * self.per + self.k)

    def end(self):
        assert self.k == self.per, (self.k, self.per)


def gnn_kernel(nc, x, adj, w0, a0, w1, a_src, a_dst, beta, w_out, out):
    ctx = ExitStack()
    with ctx:
        def sb(name, shape, dt=F32, where=ctx):
            return where.enter_context(nc.sbuf_tensor(name, shape, dt))

        def sem(name):
            return ctx.enter_context(nc.semaphore(name))

        x1_dram = nc.dram_tensor("x1_scratch", (BS, N, D), F32, kind="Internal").ap()
        es_dram = nc.dram_tensor("es_scratch", (BS, NT * H, P), F32, kind="Internal").ap()

        ident = sb("ident", [P, P])
        identb = sb("identb", [P, P], BF16)
        ones_col = sb("ones_col", [P, 1], BF16)
        Gt = sb("Gt", [P, NT, N], FP8)
        GtN = sb("GtN", [P, NT, N], FP8)
        emptyb = sb("emptyb", [P, N], BF16)
        W0 = sb("W0", [P, D + 2])
        W1 = sb("W1", [P, D + 2 * H])
        WoT = sb("WoT", [P, D])
        xp = sb("xp", [P, NT, NH, KW])
        edes = sb("edes", [P, NT, NH])
        e_pad = sb("e_pad", [P, P])
        e_s = e_pad[:, 0:NT * H].rearrange("p (t h) -> p t h", h=H)
        csum3 = sb("csum3", [P, NH, VW, 3], BF16)
        csr = sb("csr", [1, D])
        crow0 = [sb(f"crow0{q}", [P, 3, D + 1], BF16) for q in range(2)]
        BD = sb("BD", [P, NT, NH, 2])
        R1 = sb("R1", [P, NT, NH])
        cmps = sb("cmps", [P, NH, 2, NT])
        cmph = [sb(f"cmph{q}", [P, 2, NT]) for q in range(4)]
        edp = sb("edp", [P, NT, H])
        esm = sb("esm", [P, NT, H])
        Dexp = sb("Dexp", [P, NT, H])
        m8 = sb("m8", [P, H])
        M8 = sb("M8", [P, H])
        lp = sb("lp", [P, 1])
        tiny = sb("tiny", [P, 8])
        stats = sb("stats", [P, NT, 6])
        mv = sb("mv", [P, NT, 2])
        rstd = sb("rstd", [P, NT])
        rstd_e = sb("rstd_e", [P, NT])
        nmean = sb("nmean", [P, NT])
        nshift = sb("nshift", [P, NT])
        zeros = sb("zeros", [P, NT])
        lneps = sb("lneps", [P, NT])
        mhalf = sb("mhalf", [P, NT])
        rden = sb("rden", [P, NT * H])
        idle = sb("idle", [P, 1])
        idle_v = sb("idle_v", [P, 1])

        L0 = ExitStack()
        Pt = [sb(f"Pt{q}", [P, NT, N], F32, L0) for q in range(2)]
        xin = [sb(f"xin{q}", [P, NT, D], F32, L0) for q in range(2)]
        Rb = sb("Rb", [P, N], F32, L0)
        hA = [sb(f"hA{q}", [P, NT, D + 1], F32, L0) for q in range(2)]
        xres0 = [sb("xres00", [P, NT, D], F32, L0)]
        hp = [sb("hp0", [P, NT, D], F32, L0)]
        xres0 += [sb("xres01", [P, NT, D], F32, L0)]
        hp += [sb("hp1", [P, NT, D], F32, L0)]
        x1b = sb("x1b", [P, NT, D], F32, L0)
        xT = sb("xT", [P, N], F32, L0)
        et = sb("et", [P, NT, D], F32, L0)
        es_row = sb("es_row", [NT * H, P], F32, L0)
        csx = [sb(f"csx_{q}", [P, 1], F32, L0) for q in range(2)]
        csx1 = sb("csx_l1", [P, 1], F32, L0)
        s12 = sb("s12", [P, NT, 2], F32, L0)
        s2p = sb("s2p", [P, NT], F32, L0)
        s1p = sb("s1p", [P, NT], F32, L0)
        smax = sb("smax", [P, 2], F32, L0)
        bd = [sb(f"bd{q}", [P, 3 * NT], F32, L0) for q in range(2)]
        adj_in = [Pt[1][:, s, :].bitcast(I32) for s in range(4)]
        Gi = [Pt[1][:, 4, s * 512:(s + 1) * 512].bitcast(BF16) for s in range(2)]
        wraw = Pt[1][:, 5, 0:P]
        woraw = Pt[1][:, 5, P:2 * P]
        asb = Pt[1][:, 5, 2 * P:3 * P]
        adb = Pt[1][:, 5, 3 * P:4 * P]
        wprod = Pt[1][:, 5, 4 * P:6 * P]
        w0T = Pt[1][:, 6, 0:P]
        a21 = Pt[1][:, 6, P:P + 2]
        L0.close()

        C = [sb(f"C{q}", [P, NT, N], U8) for q in range(2)]
        srow = [sb(f"srow{q}", [P, N]) for q in range(4)]
        Hm = [sb(f"Hm{q}", [P, NT, N], FP8) for q in range(2)]
        C += [sb(f"C{q}", [P, NT, N], U8) for q in range(2, NC)]
        V = [sb(f"V{q}", [P, NT, VW, 3]) for q in range(4)]
        Sb = sb("Sb", [P, NT, H, VW])
        xres = sb("xres", [P, NT, D])
        hT = sb("hT", [P, N])
        hc = sb("hc", [P, NT, D])
        yout = sb("yout", [P, NT, D])

        XT = ctx.enter_context(nc.psum_tensor("XT", [P, 1024], F32))
        HH = ctx.enter_context(nc.psum_tensor("HH", [P, 3, 512], F32))
        OUT = ctx.enter_context(nc.psum_tensor("OUT", [P, 3, 512], F32))
        cs0_ps = HH[0:1, 2, 260:388]
        cs1_ps = HH[0:1, 2, 300:428]
        acc = [OUT[:, 0:2, :], HH[:, 0:2, :]]
        OPb = [HH[:, 2, :], OUT[:, 2, :]]

        def third(t, w):
            return [(t[:, 0:2, 0:3 * w].rearrange("p k (t w) -> p k t w", w=w), 0, 6),
                    (t[:, 2, 0:2 * w].rearrange("p (t w) -> p t w", w=w), 6, 8)]

        adj_ld = [sem(f"adj_ld{s}") for s in range(4)]
        w_ld, const_ok = sem("w_ld"), sem("const_ok")
        gi_ok, gT_ps, gt_ok, gtn_ok = sem("gi_ok"), sem("gT_ps"), sem("gt_ok"), sem("gtn_ok")
        deg_ps, empty_ok = sem("deg_ps"), sem("empty_ok")
        wT_ps, wT_ok, wa_ps, w_ok = sem("wT_ps"), sem("wT_ok"), sem("wa_ps"), sem("w_ok")
        lp_lnk, set_lnk = sem("lp_lnk"), sem("set_lnk")
        xin_ld = [sem(f"xin_ld{q}") for q in range(2)]
        xr0_ld = [sem(f"xr0_ld{q}") for q in range(2)]
        s1_ok, hh_rd = sem("s1_ok"), sem("hh_rd")
        xT_ps, xT_ok, h_ps, s1_ps = sem("xT_ps"), sem("xT_ok"), sem("h_ps"), sem("s1_ps")
        h_ok, mx_ok, gmx_ok, s2_ok, bd_lnk, R_ok = [sem(n) for n in
            ("h_ok", "mx_ok", "gmx_ok", "s2_ok", "bd_lnk", "R_ok")]
        relu_ok, P_ok, out_ps, out_rd, min_ok, elu_ok = [sem(n) for n in
            ("relu_ok", "P_ok", "out_ps", "out_rd", "min_ok", "elu_ok")]
        rs_ok, rs1_ok = sem("rs_ok"), sem("rs1_ok")
        mv_ok, x1_ok, x1_st, x1T_ps, x1T_ok = [sem(n) for n in
            ("mv_ok", "x1_ok", "x1_st", "x1T_ps", "x1T_ok")]
        xp_ps, xp_ok, ed_ok, es_ps, es_ok, es_st = [sem(n) for n in
            ("xp_ps", "xp_ok", "ed_ok", "es_ps", "es_ok", "es_st")]
        g_lnk = sem("g_lnk")
        f_lnk, m_lnk, n_lnk, p_lnk, pm_lnk = [sem(n) for n in ("f_lnk", "m_lnk", "n_lnk", "p_lnk", "pm_lnk")]
        pad_ok, cmp_ok = sem("pad_ok"), sem("cmp_ok")
        ed_mx, ed_gmx, edp_ok, d_lnk, bexp_ok, z_lnk = [sem(n) for n in
            ("ed_mx", "ed_gmx", "edp_ok", "d_lnk", "bexp_ok", "z_lnk")]
        srow_ld = [sem(f"srow_ld{q}") for q in range(4)]
        vm_ok = sem("vm_ok")
        V_ok, v_lnk, ccmp_a, ccmp_v, hm_ok, hd_ps, red_ok = [sem(n) for n in
            ("V_ok", "v_lnk", "ccmp_a", "ccmp_v", "hm_ok", "hd_ps", "red_ok")]
        hc_ok, hT_ps, hT_ok, op_ps, y_ok, y_st, xres_ld = [sem(n) for n in
            ("hc_ok", "hT_ps", "hT_ok", "op_ps", "y_ok", "y_st", "xres_ld")]
        k_lnk, t_lnk, mv1_ok, pt_lnk = [sem(n) for n in ("k_lnk", "t_lnk", "mv1_ok", "pt_lnk")]

        x_t = x.rearrange("b (t p) d -> b p t d", p=P)
        x1_t = x1_dram.rearrange("b (t p) d -> b p t d", p=P)
        out_t = out.rearrange("b (t p) d -> b p t d", p=P)
        adj_t = adj.rearrange("(t p) j -> t p j", p=P)
        N_W = 8

        def l0_steps(eng, body):
            body(0, 0, 0)
            body(1, 1, 0)
            with eng.Fori(0, (BS - 4) // 2) as t:
                body(t * 2 + 2, 0, t + 1)
                body(t * 2 + 3, 1, t + 1)
            body(BS - 2, 0, BS // 2 - 1)
            body(BS - 1, 1, BS // 2 - 1)

        def is_first(b):
            return isinstance(b, int) and b == 0

        def before(b, n):
            return isinstance(b, int) and b < n

        def is_last(b):
            return isinstance(b, int) and b == BS - 1

        def scalar_chunks(b, h):
            return (AC0 if is_first(b) else ACL if is_last(b) else AC)[h]

        block = ctx.enter_context(nc.Block())

        @block.sync
        def _(sp):
            sp.dma_start(wraw, w0).then_inc(w_ld, 16)
            sp.dma_start(W1[:, 0:D].rearrange("d (h f) -> d h f", h=H),
                         w1.rearrange("h d f -> d h f")).then_inc(w_ld, 16)
            for k in range(2):
                sp.dma_start(a21[:, 1 - k:2 - k], a0[k * P:(k + 1) * P, :]).then_inc(w_ld, 16)
            sp.dma_start(asb, a_src.rearrange("h f -> (h f)").partition_broadcast(P)).then_inc(w_ld, 16)
            sp.dma_start(adb, a_dst.rearrange("h f -> (h f)").partition_broadcast(P)).then_inc(w_ld, 16)
            sp.dma_start(woraw, w_out).then_inc(w_ld, 16)
            sp.dma_start(lp[:], beta.partition_broadcast(P)).then_inc(w_ld, 16)
            sp.dma_start(xin[0][:], x_t[0]).then_inc(xin_ld[0], 16)
            for t in range(NT):
                if t >= 4:
                    sp.wait_ge(gi_ok, t - 3)
                sp.dma_start(adj_in[t % 4], adj_t[t]).then_inc(adj_ld[t % 4], 16)
            sp.dma_start(xin[1][:], x_t[1]).then_inc(xin_ld[1], 16)
            for q in range(2):
                sp.dma_start(xres0[q][:], x_t[q]).then_inc(xr0_ld[q], 16)

            def load_in(b, q):
                sp.wait_ge(xT_ps, b + 1)
                sp.dma_start(xin[q][:], x_t[bass.ds(b + 2, 1)].rearrange("o p t d -> (o p) t d")
                             if not isinstance(b, int) else x_t[b + 2]).then_inc(xin_ld[q], 16)

            def load_res(b, q):
                sp.dma_start(xres0[q][:], x_t[bass.ds(b + 2, 1)].rearrange("o p t d -> (o p) t d")
                             if not isinstance(b, int) else x_t[b + 2]).then_inc(xr0_ld[q], 16)

            def store_es(b):
                sp.wait_ge(es_ok, b + 1)
                sp.dma_start(es_dram[bass.ds(b, 1)].rearrange("o k p -> (o k) p"), es_row[:]).then_inc(es_st, 16)

            def store_x1(b):
                sp.wait_ge(x1_ok, b + 1)
                sp.dma_start(x1_t[bass.ds(b, 1)].rearrange("o p t d -> (o p) t d")
                             if not isinstance(b, int) else x1_t[b], x1b[:]).then_inc(x1_st, 16)

            def step(b, q):
                if not (isinstance(b, int) and b >= BS - 2):
                    load_in(b, q)
                if not before(b, 2):
                    store_es(b - 2)
                if not is_first(b):
                    store_x1(b - 1)
                    if not is_last(b):
                        load_res(b - 1, 1 - q)

            step(0, 0)
            step(1, 1)
            with sp.Fori(0, (BS - 4) // 2) as t:
                step(t * 2 + 2, 0)
                step(t * 2 + 3, 1)
            step(BS - 2, 0)

            def load_row(b, h):
                n = b * H + h
                if not (isinstance(b, int) and n < 4):
                    sp.wait_ge(ccmp_a, n - 3)
                    sp.wait_ge(ccmp_v, n - 3)
                sp.dma_start(srow[h % 4][:].rearrange("p (t n) -> p t n", n=P),
                             es_dram.rearrange("b (t h) p -> b h t p", h=H)[bass.ds(b, 1), h, :, :]
                             .rearrange("o t p -> (o t) p")
                             .partition_broadcast(P)).then_inc(srow_ld[h % 4], 16)
                sp.dma_start(cmph[h % 4][:].rearrange("p k t -> p (k t)"),
                             cmps[:, bass.ds(n, 1), :, :].rearrange("p o k t -> p (o k t)")).then_inc(srow_ld[h % 4], 16)

            sp.wait_ge(es_st, 16)
            sp.wait_ge(cmp_ok, 1)
            sp.wait_ge(out_ps, BS - 1)
            for h in range(4):
                load_row(0, h)
            store_es(BS - 3)
            store_x1(BS - 2)
            store_es(BS - 2)
            for h in range(4, H):
                load_row(0, h)
            sp.wait_ge(es_st, 16 * (BS - 1))
            with sp.Fori(1, BS - 1) as b:
                for h in range(H):
                    load_row(b, h)
            sp.wait_ge(es_st, 16 * BS)
            for h in range(H):
                load_row(BS - 1, h)

        @block.gpsimd
        def _(pool):
            pool.memset(ident[:], 0.0).then_inc(set_lnk, 1)
            pool.wait_ge(set_lnk, 1)
            pool.affine_select(out=ident[:], in_=ident[:], compare_op=ALU.not_equal, fill=1.0, base=0,
                               pattern=[[-1, P]], channel_multiplier=1).then_inc(set_lnk, 1)
            pool.wait_ge(set_lnk, 2)
            pool.tensor_copy(identb[:], ident[:])
            pool.memset(ones_col[:], 1.0)
            pool.memset(lneps[:], LN_EPS)
            pool.memset(mhalf[:], -0.5)
            pool.memset(zeros[:], 0.0)
            pool.memset(tiny[:], 0.0).then_inc(const_ok, 1)
            for q in range(2):
                pool.memset(crow0[q][:], 0.0).then_inc(set_lnk, 1)
            pool.wait_ge(set_lnk, 4)
            for q in range(2):
                pool.memset(crow0[q][0:1, 0, D:D + 1], float(N))
                pool.memset(hA[q][:, :, D:D + 1], 1.0)
            pool.memset(xp[:, :, :, DH:KW], 1.0)
            pool.memset(e_pad[:], 0.0)
            pool.memset(emptyb[:], 0.0).then_inc(pad_ok, 1)

            pm = Links(pool, pm_lnk, 2)
            pt = Links(pool, pt_lnk, 1)

            def front(b):
                pool.wait_ge(mx_ok, b + 1)
                if not is_first(b):
                    pool.wait_ge(s1_ok, b)
                pool.tensor_tensor(idle[:], lneps[:, 0:1], lneps[:, 0:1], ALU.add)
                pool.partition_all_reduce(smax[:, 1:2], smax[:, 0:1], P, RMAX).then_inc(gmx_ok, 1)

            def rsqrt(b):
                pt.begin(b)
                pool.wait_ge(mv1_ok, b + 1)
                pt.link(pool.tensor_tensor(rstd_e[:], mv[:, :, 1], lneps[:], ALU.add))
                pool.tensor_tensor(rstd[:], rstd_e[:], mhalf[:], ALU.pow).then_inc(rs1_ok, 1)
                pt.end()

            def rsqrt_shift(b):
                pm.begin(b)
                pool.wait_ge(mv_ok, b + 1)
                if not is_first(b):
                    pool.wait_ge(x1_ok, b)
                pool.tensor_tensor(nmean[:], zeros[:], mv[:, :, 0], ALU.subtract)
                pm.link(pool.tensor_tensor(rstd_e[:], mv[:, :, 1], lneps[:], ALU.add))
                pm.link(pool.tensor_tensor(rstd[:], rstd_e[:], mhalf[:], ALU.pow))
                pool.tensor_tensor(nshift[:], nmean[:], rstd[:], ALU.mult).then_inc(rs_ok, 1)
                pm.end()

            front(0)
            pool.memset(csum3[:], 0.0).then_inc(set_lnk, 1)
            pool.wait_ge(set_lnk, 5)
            pool.memset(csum3[0:1, :, VW - 1, 0], float(N)).then_inc(pad_ok, 1)

            def table_max(b):
                pool.wait_ge(ed_mx, b + 1)
                if not is_first(b):
                    pool.wait_ge(edp_ok, b)
                pool.tensor_tensor(idle[:], lneps[:, 0:1], lneps[:, 0:1], ALU.add)
                pool.partition_all_reduce(M8[:], m8[:], P, RMAX).then_inc(ed_gmx, 1)

            def step(b, q, _):
                if not is_last(b):
                    front(b + 1)
                if is_last(b):
                    table_max(b - 2)
                if not is_first(b):
                    rsqrt_shift(b - 1)
                if not before(b, 2) and not is_last(b):
                    table_max(b - 2)
            l0_steps(pool, step)

            vl = Links(pool, v_lnk, 1)

            def split_values(b, h):
                n = b * H + h
                vl.begin(n)
                pool.wait_ge(vm_ok, n + 1)
                v = V[h % 4]
                hi = v[:].bitcast(BF16).rearrange("p t f (k u) -> p (t f) k u", u=2)[:, :, :, 1]
                w = v[:].rearrange("p t f k -> p (t f) k")
                vl.link(pool.tensor_tensor(w[:, :, 1], w[:, :, 0], hi[:, :, 0], ALU.subtract))
                pool.tensor_tensor(w[:, :, 2], w[:, :, 1], hi[:, :, 1], ALU.subtract).then_inc(V_ok, 1)
                vl.end()

            def l1_batch(b):
                for h in range(H):
                    split_values(b, h)
                    if is_first(b):
                        if h == 1:
                            table_max(BS - 2)
                        if h == T_FINISH:
                            rsqrt_shift(BS - 1)
                        if h == H - 2:
                            table_max(BS - 1)
                    elif h == H - 1:
                        rsqrt(b - 1)
            l1_batch(0)
            with pool.Fori(1, BS) as b:
                l1_batch(b)
            rsqrt(BS - 1)

        @block.scalar
        def _(act):
            a = nc.scalar
            act.wait_ge(w_ld, 16 * N_W)
            act.wait_ge(const_ok, 1)

            def chain(ins, k):
                ins.then_inc(lp_lnk, 1)
                act.wait_ge(lp_lnk, k)
            chain(a.activation(tiny[:, 0:1], lp[:], ACT.Abs), 1)
            chain(a.activation(tiny[:, 1:2], tiny[:, 0:1], ACT.Exp, scale=-1.0), 2)
            chain(a.activation(tiny[:, 2:3], tiny[:, 1:2], ACT.Ln, bias=1.0), 3)
            chain(a.activation(tiny[:, 3:4], lp[:], ACT.Relu, bias=0.0), 4)
            chain(a.activation(tiny[:, 5:6], tiny[:, 4:5], ACT.Ln, bias=1.0 + LOG_EPS), 5)

            def negate_mask(t0, t1):
                a.activation(GtN[:, t0:t1, :], Gt[:, t0:t1, :], ACT.Copy, scale=-1.0, saturate=False)\
                 .then_inc(gtn_ok, 1)

            bdl = Links(act, bd_lnk, 3)

            def copy_xT(b, q):
                act.wait_ge(xT_ps, b + 1)
                a.activation(xT[:], XT[:], ACT.Copy, accum_out=csx[q][:]).then_inc(xT_ok, 1)

            def front(b, q):
                act.wait_ge(hh_rd, b + 1)
                for v, t0, t1 in third(HH, D + 2):
                    last = a.activation(hA[q][:, t0:t1, 0:D] if t0 else
                                        hA[q][:, t0:t1, 0:D].rearrange("p (k t) d -> p k t d", k=2),
                                        v[..., 0:D], ACT.Copy)
                last.then_inc(h_ok, 1)
                if not before(b, 2):
                    elu(b - 2)
                act.wait_ge(s2_ok, b + 1)
                bdl.begin(b)
                bdl.link(a.activation(bd[q][:, 0:NT], s2p[:], ACT.Exp))
                bdl.link(a.activation(bd[q][:, NT:2 * NT], s2p[:], ACT.Exp, scale=SLOPE))
                bdl.link(a.activation(bd[q][:, 2 * NT:], bd[q][:, NT:2 * NT], ACT.Copy, scale=-1.0))
                bdl.end()
                act.wait_ge(s1_ps, b + 1)
                a.activation(Rb[:], XT[:], ACT.Exp, scale=1.0 - SLOPE).then_inc(R_ok, 1)

            def scores(b, q, between):
                act.wait_ge(R_ok, b + 1)
                if not (isinstance(b, int) and b < 2):
                    act.wait_ge(out_ps, b - 1)
                for c in range(NT):
                    a.activation(Pt[q][:, c, :], Rb[:], ACT.Relu, scale=bd[q][:, c:c + 1],
                                 bias=bd[q][:, 2 * NT + c:2 * NT + c + 1]).then_inc(relu_ok, 1)
                    if between and c in between:
                        between[c]()

            def copy_x1T(b):
                act.wait_ge(x1T_ps, b + 1)
                a.activation(xT[:], XT[:], ACT.Copy, accum_out=csx1[:]).then_inc(x1T_ok, 1)

            def copy_proj(b):
                act.wait_ge(ed_ok, b + 1)
                for t in range(0, NT, 3):
                    w = min(3, NT - t)
                    last = a.activation(xp[:, t:t + w, bass.ds(b * H, H), 0:DH],
                                        HH[:, t // 3, 0:w * (D + 2 * H)].rearrange("p (t w) -> p t w", t=w)[:, :, 0:D]
                                        .rearrange("p t (h f) -> p t h f", h=H), ACT.Copy)
                last.then_inc(xp_ok, 1)

            def copy_es(b):
                act.wait_ge(es_ps, b + 1)
                if not is_first(b):
                    act.wait_ge(es_st, b * 16)
                a.activation(es_row[:], HH[0:NT * H, 0, 0:P], ACT.Copy).then_inc(es_ok, 1)

            def normalise(b, q):
                act.wait_ge(rs_ok, b + 1)
                if not is_first(b):
                    act.wait_ge(x1_st, b * 16)
                    act.wait_ge(x1T_ps, b)
                for t in range(NT):
                    last = a.activation(x1b[:, t, :], hp[q][:, t, :], ACT.Identity, scale=rstd[:, t:t + 1],
                                        bias=nshift[:, t:t + 1])
                last.then_inc(x1_ok, 1)

            def elu(b):
                act.wait_ge(min_ok, b + 1)
                a.activation(et[:], et[:], ACT.Exp).then_inc(elu_ok, 1)

            def compare(b, h):
                n = b * H + h
                act.wait_ge(srow_ld[h % 4], (b * 2 + h // 4 + 1) * 32)
                if not (isinstance(b, int) and n < NC):
                    act.wait_ge(hm_ok, n - NC + 1)
                for c in range(scalar_chunks(b, h)):
                    last = a.activation(C[h % NC][:, c, :], srow[h % 4][:], ACT.Sigmoid, scale=STEEP,
                                        bias=cmph[h % 4][:, 0, c:c + 1])
                last.then_inc(ccmp_a, 1)

            dl = Links(act, d_lnk, 1)

            def tables(b):
                dl.begin(b)
                act.wait_ge(edp_ok, b + 1)
                bh = bass.ds(b * H, H)
                dl.link(a.activation(Dexp[:], edp[:], ACT.Exp, scale=SLOPE, bias=lp[:]))
                a.activation(BD[:, :, bh, 0], edp[:], ACT.Exp, bias=lp[:])
                a.activation(BD[:, :, bh, 1], Dexp[:], ACT.Copy, scale=-1.0)
                a.activation(R1[:, :, bh], esm[:], ACT.Exp, scale=1.0 - SLOPE).then_inc(bexp_ok, 1)
                dl.end()

            def step(b, q, _):
                if is_last(b):
                    elu(b - 1)
                    copy_x1T(b - 2)
                    copy_proj(b - 2)
                    copy_es(b - 2)
                    tables(b - 2)
                    normalise(b - 1, 1 - q)
                    compare(0, 0)
                    copy_x1T(b - 1)
                    compare(0, 1)
                    copy_proj(b - 1)
                    copy_es(b - 1)
                    return
                front(b + 1, 1 - q)
                between = {}
                if not before(b, 2):
                    between[ACT_X1T] = lambda: copy_x1T(b - 2)
                    between[ACT_PROJ] = lambda: copy_proj(b - 2)
                scores(b + 1, 1 - q, between)
                if before(b, 2):
                    negate_mask(b * 4, b * 4 + 4)
                if not (isinstance(b, int) and b >= BS - 2):
                    copy_xT(b + 2, q)
                if not before(b, 2):
                    copy_es(b - 2)
                    tables(b - 2)
                if not is_first(b):
                    normalise(b - 1, 1 - q)

            copy_xT(0, 0)
            front(0, 0)
            scores(0, 0, None)
            copy_xT(1, 1)
            act.wait_ge(gt_ok, NT)
            act.wait_ge(w_ok, 1)
            act.wait_ge(gT_ps, NT)
            l0_steps(act, step)
            act.wait_ge(out_ps, BS)


            def copy_hT(b):
                act.wait_ge(hT_ps, b + 1)
                a.activation(hT[:], XT[:], ACT.Copy).then_inc(hT_ok, 1)

            def store_y(b):
                act.wait_ge(y_ok, b + 1)
                act.dma_start(out_t[b] if isinstance(b, int) else
                              out_t[bass.ds(b, 1)].rearrange("o p t d -> (o p) t d"), yout[:]).then_inc(y_st, 16)

            def load_res(b):
                act.dma_start(xres[:], x1_t[b] if isinstance(b, int) else
                              x1_t[bass.ds(b, 1)].rearrange("o p t d -> (o p) t d")).then_inc(xres_ld, 16)

            def l1_batch(b):
                for h in range(2 if is_first(b) else 0, H):
                    compare(b, h)
                    if is_first(b):
                        if h == T_FINISH:
                            elu(BS - 1)
                            tables(BS - 2)
                        if h == T_X1T + 1:
                            normalise(BS - 1, 1)
                        if h == T_X1T + 2:
                            copy_x1T(BS - 1)
                            act.dma_start(x1_t[BS - 1], x1b[:]).then_inc(x1_st, 16)
                        if h == T_PROJ + 2:
                            copy_proj(BS - 1)
                            copy_es(BS - 1)
                            act.wait_ge(es_ok, BS)
                            act.dma_start(es_dram[BS - 1], es_row[:]).then_inc(es_st, 16)
                    if isinstance(b, int) and b == 1 and h == 2:
                        tables(BS - 1)

                    if h == 3 and not is_first(b):
                        if not before(b, 2):
                            store_y(b - 2)
                        load_res(b - 1)
                    if h == 5 and not is_first(b):
                        copy_hT(b - 1)
            l1_batch(0)
            act.wait_ge(x1_st, 16 * BS)
            l1_batch(1)
            with act.Fori(2, BS - 1) as b:
                l1_batch(b)
            l1_batch(BS - 1)
            store_y(BS - 2)
            load_res(BS - 1)
            copy_hT(BS - 1)
            store_y(BS - 1)
            act.wait_ge(y_st, 16 * BS)

        @block.vector
        def _(dve):
            v = nc.vector
            dve.wait_ge(const_ok, 1)
            dve.wait_ge(w_ld, 16 * N_W)
            for k, (vec, col) in enumerate(((adb, D), (asb, D + H))):
                last = v.tensor_tensor(wprod[:, k * D:(k + 1) * D], W1[:, 0:D], vec, ALU.mult)
            last.then_inc(z_lnk, 1)
            dve.wait_ge(z_lnk, 1)
            v.tensor_reduce(W1[:, D:D + 2 * H], wprod.rearrange("p (h f) -> p h f", f=DH), AX.X, ALU.add)
            dve.wait_ge(wT_ps, 1)
            v.tensor_copy(w0T, XT[:, 0:P])
            v.tensor_copy(WoT[:], XT[:, P:2 * P])
            v.tensor_copy(W0[:, 0:D], wraw).then_inc(wT_ok, 1)
            dve.wait_ge(wa_ps, 1)
            v.tensor_copy(W0[:, D:D + 2], XT[:, 2 * P:2 * P + 2]).then_inc(z_lnk, 1)
            dve.wait_ge(lp_lnk, 5)
            v.tensor_tensor(tiny[:, 6:7], tiny[:, 2:3], tiny[:, 3:4], ALU.add).then_inc(z_lnk, 1)
            dve.wait_ge(z_lnk, 3)
            v.tensor_tensor(lp[:], tiny[:, 6:7], tiny[:, 5:6], ALU.mult).then_inc(w_ok, 1)
            def mask_copy(t):
                dve.wait_ge(gT_ps, t + 1)
                v.tensor_copy(Gt[:, :, t * P:(t + 1) * P],
                              OUT[:, t % 2, :].bitcast(BF16).rearrange("p (c i) -> p c i", c=NT), saturate=False).then_inc(gt_ok, 1)

            def mask_tiles(t0, t1):
                for t in range(t0, t1):
                    dve.wait_ge(adj_ld[t % 4], 16 * (t // 4 + 1))
                    if t >= 2:
                        dve.wait_ge(gT_ps, t - 1)
                    v.tensor_scalar(Gi[t % 2], adj_in[t % 4], 0, EDGE, ALU.is_gt, ALU.mult).then_inc(gi_ok, 1)
                    if t >= 1:
                        mask_copy(t - 1)

            def empty_rows():
                dve.wait_ge(deg_ps, 1)
                dve.wait_ge(pad_ok, 1)
                v.tensor_scalar(emptyb[0:1, :], OUT[0:1, 0:2, :].rearrange("p k n -> p (k n)"), 0.0, EDGE, ALU.is_equal, ALU.mult).then_inc(empty_ok, 1)

            def three_parts(links, src, rest, hi, mid, lo):
                links.link(v.tensor_copy(hi, src))
                links.link(v.tensor_tensor(rest, src, hi, ALU.subtract))
                links.link(v.tensor_copy(mid, rest))
                return v.tensor_tensor(lo, rest, mid, ALU.subtract)

            fl = Links(dve, f_lnk, 4)
            pl = Links(dve, p_lnk, 3)
            ml = Links(dve, m_lnk, 1)
            nl = Links(dve, n_lnk, 3)
            gl = Links(dve, g_lnk, 1)

            def front(b, q):
                fl.begin(b)
                dve.wait_ge(h_ps, b + 1)
                if not is_first(b):
                    dve.wait_ge(gmx_ok, b)
                for hv, t0, t1 in third(HH, D + 2):
                    s = s12[:, t0:t1, :]
                    last = v.tensor_copy(s if t0 else s.rearrange("p (k t) c -> p k t c", k=2), hv[..., D:D + 2])
                fl.link(last)
                v.tensor_reduce(smax[:, 0:1], s12[:, :, 0], AX.X, ALU.max).then_inc(mx_ok, 1)
                if not (isinstance(b, int) and b < 2):
                    dve.wait_ge(out_ps, b - 1)
                else:
                    dve.wait_ge(pad_ok, 1)
                cr = crow0[q][0:1, :, 0:D]
                three_parts(fl, cs0_ps, csr[:], cr[:, 0], cr[:, 1], cr[:, 2]).then_inc(hh_rd, 1)
                dve.wait_ge(gmx_ok, b + 1)
                if not is_first(b):
                    dve.wait_ge(s1_ps, b)
                    dve.wait_ge(R_ok, b)
                v.tensor_scalar(s1p[:], s12[:, :, 1], smax[:, 1:2], CAP, ALU.add, ALU.min).then_inc(s1_ok, 1)
                v.tensor_scalar(s2p[:], s12[:, :, 0], smax[:, 1:2], None, ALU.subtract).then_inc(s2_ok, 1)
                fl.end()

            def scores(b, q, between):
                for c in range(NT):
                    if between and c in between:
                        between[c]()
                    dve.wait_ge(relu_ok, b * NT + c + 1)
                    v.scalar_tensor_tensor(Pt[q][:, c, :], Pt[q][:, c, :], bd[q][:, NT + c:NT + c + 1],
                                           Gt[:, c, :].bitcast(U8), ALU.add, ALU.mult).then_inc(P_ok, 1)

            def layernorm_stats(links, y, done):
                for t in range(NT):
                    last = v.bn_stats(stats[:, t, :], y[t])
                links.link(last)
                v.tensor_copy(idle_v[:], lneps[:, 0:1])
                for t in range(NT):
                    last = v.bn_aggr(mv[:, t, :], stats[:, t, :])
                last.then_inc(done, 1)

            def divide(b, q):
                ml.begin(b)
                dve.wait_ge(out_ps, b + 1)
                if not before(b, 2):
                    dve.wait_ge(x1_ok, b - 1)
                for o, t0, t1 in third(OUT, D + 1):
                    r = rden[:, t0:t1]
                    last = v.reciprocal(r if t0 else r.rearrange("p (k t) -> p k t", k=2), o[..., D])
                ml.link(last)
                for o, t0, t1 in third(OUT, D + 1):
                    if t0:
                        last = v.tensor_tensor(hp[q][:, t0:t1, :], o[..., 0:D],
                                               rden[:, t0:t1].unsqueeze(2).to_broadcast([P, t1 - t0, D]), ALU.mult)
                    else:
                        v.tensor_tensor(hp[q][:, 0:6, :].rearrange("p (k t) d -> p k t d", k=2), o[..., 0:D],
                                        rden[:, 0:6].rearrange("p (k t) -> p k t", k=2).unsqueeze(3)
                                        .to_broadcast([P, 2, 3, D]), ALU.mult)
                last.then_inc(out_rd, 1)
                dve.wait_ge(out_rd, b + 1)
                if not is_first(b):
                    dve.wait_ge(n_lnk, b * 3)
                v.tensor_scalar(et[:], hp[q][:], 0.0, None, ALU.min).then_inc(min_ok, 1)
                ml.end()

            def finish(b, q, half):
                nl.begin(b)
                dve.wait_ge(xr0_ld[q], (half + 1) * 16)
                nl.link(v.scalar_tensor_tensor(hp[q][:], hp[q][:], 0.0, xres0[q][:], ALU.max, ALU.add))
                dve.wait_ge(elu_ok, b + 1)
                nl.link(v.scalar_tensor_tensor(hp[q][:], et[:], -1.0, hp[q][:], ALU.add, ALU.add))
                layernorm_stats(nl, [hp[q][:, t, :] for t in range(NT)], mv_ok)
                nl.end()

            def proj(b):
                pl.begin(b)
                dve.wait_ge(xp_ps, b + 1)
                if not is_first(b):
                    dve.wait_ge(es_ps, b)
                for hv, t0, t1 in third(HH, D + 2 * H):
                    for k, o in enumerate((edes[:, t0:t1, bass.ds(b * H, H)], e_s[:, t0:t1, :])):
                        v.tensor_copy(o if t0 else o.rearrange("p (k t) h -> p k t h", k=2),
                                      hv[..., D + k * H:D + (k + 1) * H])
                if is_first(b):
                    dve.wait_ge(pad_ok, 2)
                c3 = [csum3[0:1, bass.ds(b * H, H), KW:VW - 1, k] for k in range(3)]
                three_parts(pl, cs1_ps.rearrange("o (h f) -> o h f", h=H),
                            csr[:].rearrange("o (h f) -> o h f", h=H), *c3).then_inc(ed_ok, 1)
                edn = edes[:, :, bass.ds(b * H, H)].rearrange("p t e -> p e t")
                if not is_first(b):
                    dve.wait_ge(ed_gmx, b)
                v.tensor_copy(idle_v[:], lneps[:, 0:1])
                v.tensor_reduce(m8[:], edn, AX.X, ALU.max).then_inc(ed_mx, 1)
                v.tensor_scalar(
cmps[:, bass.ds(b * H, H), 0, :], edn, STEEP, None, ALU.mult)
                v.tensor_scalar(cmps[:, bass.ds(b * H, H), 1, :], edn, -1.0, None, ALU.mult).then_inc(cmp_ok, 1)
                pl.end()

            def tables(b):
                dve.wait_ge(ed_gmx, b + 1)
                if not is_first(b):
                    dve.wait_ge(bexp_ok, b)
                bh = bass.ds(b * H, H)
                mb = M8[:].unsqueeze(1).to_broadcast([P, NT, H])
                gl.begin(b)
                v.tensor_tensor(edp[:], edes[:, :, bh], mb, ALU.subtract)
                gl.link(v.tensor_tensor(esm[:], e_s, mb, ALU.add))
                v.tensor_scalar(esm[:], esm[:], CAP, None, ALU.min).then_inc(edp_ok, 1)
                gl.end()

            def step(b, q, half):
                if is_last(b):
                    finish(b - 1, 1 - q, half + q - 1)
                    proj(b - 2)
                    tables(b - 2)
                    compare(0, 0)
                    compare(0, 1)
                    values(0, 0)
                    values(0, 1)
                    proj(b - 1)
                    dve.wait_ge(out_ps, BS)
                    mask(0, 0)
                    divide(b, q)
                    tables(b - 1)
                    return
                if not is_first(b):
                    front(b + 1, 1 - q)
                    finish(b - 1, 1 - q, half + q - 1)
                between = {}
                if not before(b, 2):
                    between[DVE_PROJ] = lambda: proj(b - 2)
                scores(b + 1, 1 - q, between)
                if not before(b, 2):
                    tables(b - 2)
                divide(b, q)

            def compare(b, h):
                n = b * H + h
                dve.wait_ge(srow_ld[h % 4], (b * 2 + h // 4 + 1) * 32)
                if not (isinstance(b, int) and n < NC):
                    dve.wait_ge(hm_ok, n - NC + 1)
                for c in range(scalar_chunks(b, h), NT):
                    last = v.tensor_scalar(C[h % NC][:, c, :], srow[h % 4][:], cmph[h % 4][:, 1, c:c + 1], None,
                                           ALU.is_gt)
                last.then_inc(ccmp_v, 1)

            def values(b, h):
                n = b * H + h
                if h == 0:
                    dve.wait_ge(xp_ok, b + 1)
                    dve.wait_ge(bexp_ok, b + 1)
                if not (isinstance(b, int) and n < 4):
                    dve.wait_ge(hd_ps, n - 3)
                v.tensor_tensor(V[h % 4][:, :, :, 0].rearrange("p t (k f) -> p t k f", k=2),
                                xp[:, :, bass.ds(n, 1), :].to_broadcast([P, NT, 2, KW]),
                                BD[:, :, bass.ds(n, 1), :].rearrange("p t o k -> p t (o k)").unsqueeze(3)
                                .to_broadcast([P, NT, 2, KW]), ALU.mult).then_inc(vm_ok, 1)

            def mask(b, h):
                n = b * H + h
                dve.wait_ge(ccmp_a, n + 1)
                dve.wait_ge(ccmp_v, n + 1)
                if not (isinstance(b, int) and n < 2):
                    dve.wait_ge(hd_ps, n - 1)
                v.scalar_tensor_tensor(Hm[h % 2][:].rearrange("p t n -> p (t n)").bitcast(I32),
                                       C[h % NC][:].rearrange("p t n -> p (t n)").bitcast(I32), EDGE_SHIFT,
                                       Gt[:].rearrange("p t n -> p (t n)").bitcast(I32),
                                       ALU.logical_shift_left, ALU.bitwise_and).then_inc(hm_ok, 1)

            mask_tiles(0, 3)
            front(0, 0)
            mask_tiles(3, NT)
            mask_copy(NT - 1)
            dve.wait_ge(gt_ok, NT)
            scores(0, 0, {4: empty_rows, 6: lambda: front(1, 1)})
            l0_steps(dve, step)
            kl = Links(dve, k_lnk, 3)
            tl = Links(dve, t_lnk, 1)

            def parts(b, h):
                n = b * H + h
                dve.wait_ge(hd_ps, n + 1)
                if h == 0 and not is_first(b):
                    dve.wait_ge(hc_ok, b)
                v.tensor_reduce(Sb[:, :, h, :].rearrange("p (k t) c -> p k t c", k=2),
                                acc[h % 2][:, :, 0:4 * VW * 3].rearrange("p k (t c s) -> p k t c s", s=3, c=VW),
                                AX.X, ALU.add).then_inc(red_ok, 1)

            def combine(b):
                kl.begin(b)
                dve.wait_ge(red_ok, (b + 1) * H)
                if not is_first(b):
                    dve.wait_ge(hT_ps, b)
                r = R1[:, :, bass.ds(b * H, H)].unsqueeze(3).to_broadcast([P, NT, H, KW])
                kl.link(v.tensor_tensor(Sb[:, :, :, 0:KW], Sb[:, :, :, 0:KW], r, ALU.mult))
                kl.link(v.tensor_tensor(Sb[:, :, :, 0:KW], Sb[:, :, :, 0:KW], Sb[:, :, :, KW:VW], ALU.add))
                kl.link(v.reciprocal(rden[:].rearrange("p (t h) -> p t h", h=H), Sb[:, :, :, DH]))
                v.tensor_tensor(hc[:].rearrange("p t (h f) -> p t h f", h=H), Sb[:, :, :, 0:DH],
                                rden[:].rearrange("p (t h) -> p t h", h=H).unsqueeze(3)
                                .to_broadcast([P, NT, H, DH]), ALU.mult).then_inc(hc_ok, 1)
                kl.end()

            y1 = [OPb[t // 4][:, (t % 4) * D:(t % 4 + 1) * D] for t in range(NT)]

            def finish1(b):
                tl.begin(b)
                dve.wait_ge(op_ps, b + 1)
                layernorm_stats(tl, y1, mv1_ok)
                tl.end()

            def normalise1(b):
                dve.wait_ge(rs1_ok, b + 1)
                if not is_first(b):
                    dve.wait_ge(y_st, b * 16)
                for t in range(NT):
                    last = v.tensor_scalar(yout[:, t, :], y1[t], mv[:, t, 0:1], rstd[:, t:t + 1],
                                           ALU.subtract, ALU.mult)
                last.then_inc(y_ok, 1)

            def l1_batch(b):
                for h in range(1, H + 1):
                    if is_last(b) and h == H:
                        break
                    bb, hh = (b, h) if h < H else (b + 1, 0)
                    if not (is_last(b) and h == H - 1):
                        compare(*((bb, hh + 1) if hh + 1 < H else (b + 1, 0)))
                    if h >= 2:
                        parts(b, h - 2)
                    elif not is_first(b):
                        parts(b - 1, H - 1)
                    mask(bb, hh)
                    if not (is_last(b) and h + 2 >= H):
                        values(*((b, h + 2) if h + 2 < H else (b + 1, h + 2 - H)))
                    if is_first(b):
                        if h == T_FINISH:
                            finish(BS - 1, 1, BS // 2 - 1)
                        if h == T_PROJ + 1:
                            proj(BS - 1)
                        if h == H - 1:
                            tables(BS - 1)
                    if not is_first(b):
                        if h == 1:
                            combine(b - 1)
                        if h == DVE_FINISH1:
                            finish1(b - 1)
                        if h == DVE_NORM1:
                            normalise1(b - 1)

            values(0, 2)
            l1_batch(0)
            with dve.Fori(1, BS - 1) as b:
                l1_batch(b)
            l1_batch(BS - 1)
            parts(BS - 1, H - 2)
            parts(BS - 1, H - 1)
            combine(BS - 1)
            finish1(BS - 1)
            normalise1(BS - 1)

        @block.tensor
        def _(pe):
            mm = nc.tensor.matmul
            pe.wait_ge(const_ok, 1)
            pe.wait_ge(w_ld, 16 * N_W)
            nc.tensor.transpose(XT[:, 0:P], wraw, ident[:])
            nc.tensor.transpose(XT[:, P:2 * P], woraw, ident[:]).then_inc(wT_ps, 1)
            pe.wait_ge(wT_ok, 1)
            mm(XT[:, 2 * P:2 * P + 2], w0T, a21, start=True, stop=True).then_inc(wa_ps, 1)
            def tile(t, ps, w):
                return ps[:, t // 3, (t % 3) * w:(t % 3 + 1) * w]

            def transpose_x(b, q, half):
                pe.wait_ge(xin_ld[q], (half + 1) * 16)
                if not is_first(b):
                    pe.wait_ge(R_ok, b)
                for t in range(NT):
                    last = nc.tensor.transpose(XT[:, t * P:(t + 1) * P], xin[q][:, t, :], ident[:])
                last.then_inc(xT_ps, 1)

            def front(b, q):
                pe.wait_ge(xT_ok, b + 1)
                if not is_first(b):
                    pe.wait_ge(h_ok, b)
                if not before(b, 4):
                    pe.wait_ge(es_ok, b - 3)
                mm(cs0_ps, csx[q][:], W0[:, 0:D], start=True, stop=True)
                for t in range(NT):
                    last = mm(tile(t, HH, D + 2), xT[:, t * P:(t + 1) * P], W0[:], start=True, stop=True)
                last.then_inc(h_ps, 1)

            def spread_s1(b):
                pe.wait_ge(s1_ok, b + 1)
                for t in range(NT):
                    last = nc.tensor.transpose(XT[:, t * P:(t + 1) * P],
                                               s1p[:, t:t + 1].to_broadcast([P, P]), ident[:])
                last.then_inc(s1_ps, 1)

            def products(b, q, t0, t1):
                if t0 == 0:
                    pe.wait_ge(P_ok, (b + 1) * NT)
                    pe.wait_ge(h_ok, b + 1)
                    if is_first(b):
                        pe.wait_ge(empty_ok, 1)
                    else:
                        pe.wait_ge(out_rd, b)
                for t in range(t0, t1):
                    o = tile(t, OUT, D + 1)
                    for c in range(NT):
                        mm(o, Pt[q][:, c, t * P:(t + 1) * P], hA[q][:, c, :], start=c == 0, stop=False)
                    for k in range(3):
                        last = mm(o, emptyb[:, t * P:(t + 1) * P], crow0[q][:, k, :], start=False, stop=k == 2)
                if t1 == NT:
                    last.then_inc(out_ps, 1)

            def transpose_x1(b, fronts):
                pe.wait_ge(x1_ok, b + 1)
                pe.wait_ge(R_ok, fronts)
                pe.wait_ge(h_ok, fronts)
                for t in range(NT):
                    last = nc.tensor.transpose(XT[:, t * P:(t + 1) * P], x1b[:, t, :], ident[:])
                last.then_inc(x1T_ps, 1)

            def proj(b):
                pe.wait_ge(x1T_ok, b + 1)
                mm(cs1_ps, csx1[:], W1[:, 0:D], start=True, stop=True)
                for t in range(NT):
                    last = mm(tile(t, HH, D + 2 * H), xT[:, t * P:(t + 1) * P], W1[:], start=True, stop=True)
                last.then_inc(xp_ps, 1)

            def transpose_es(b):
                pe.wait_ge(ed_ok, b + 1)
                pe.wait_ge(xp_ok, b + 1)
                nc.tensor.transpose(HH[:, 0, 0:P], e_pad[:], ident[:])\
                  .then_inc(es_ps, 1)

            def step(b, q, half):
                if is_last(b):
                    products(b, q, 0, 1)
                    transpose_x1(b - 2, BS)
                    products(b, q, 1, 2)
                    pe.wait_ge(es_ok, b - 2)
                    proj(b - 2)
                    products(b, q, 2, 3)
                    transpose_es(b - 2)
                    products(b, q, 3, PE_LAST)
                    transpose_x1(b - 1, BS)
                    products(b, q, PE_LAST, NT - 1)
                    pe.wait_ge(es_ok, b - 1)
                    proj(b - 1)

                    products(b, q, NT - 1, NT)
                    transpose_es(b - 1)
                    return
                front(b + 1, 1 - q)
                if is_first(b):
                    spread_s1(1)
                    products(0, 0, 0, PE_X1T)
                else:
                    products(b, q, 0, 1)
                    spread_s1(b + 1)
                    products(b, q, 1, PE_X1T)
                if not before(b, 2):
                    transpose_x1(b - 2, BS if is_last(b) else b + 2)
                products(b, q, PE_X1T, PE_X1T + 1)
                if not before(b, 2):
                    proj(b - 2)
                products(b, q, PE_X1T + 1, NT - 1)
                if not (isinstance(b, int) and b >= BS - 2):
                    transpose_x(b + 2, q, half + 1)
                if not before(b, 2):
                    transpose_es(b - 2)
                products(b, q, NT - 1, NT)

            pe.wait_ge(w_ok, 1)

            def mask_transposes(t0, t1):
                for t in range(t0, t1):
                    pe.wait_ge(gi_ok, t + 1)
                    if t >= 2:
                        pe.wait_ge(gt_ok, t - 1)
                    for c in range(NT):
                        last = nc.tensor.transpose(OUT[:, t % 2, :].bitcast(BF16)[:, c * P:(c + 1) * P],
                                                   Gi[t % 2][:, c * P:(c + 1) * P], identb[:])
                    last.then_inc(gT_ps, 1)

            transpose_x(0, 0, 0)
            mask_transposes(0, 2)
            front(0, 0)
            mask_transposes(2, 3)
            spread_s1(0)
            mask_transposes(3, NT)
            transpose_x(1, 1, 0)
            pe.wait_ge(gt_ok, NT)
            for k in range(2):
                for c in range(NT):
                    last = mm(OUT[0:1, k, :], ones_col[:], Gt[:, c, k * 512:(k + 1) * 512],
                              start=c == 0, stop=c == NT - 1)
            last.then_inc(deg_ps, 1)
            l0_steps(pe, step)

            pe.wait_ge(out_rd, BS)
            pe.wait_ge(gtn_ok, 2)

            def head(b, h):
                n = b * H + h
                pe.wait_ge(hm_ok, n + 1)
                pe.wait_ge(V_ok, n + 1)
                if not (isinstance(b, int) and n < 2):
                    pe.wait_ge(red_ok, n - 1)
                hi = V[h % 4][:].bitcast(BF16).rearrange("p t f (k u) -> p t (f k) u", u=2)[:, :, :, 1]
                csn = csum3[:, bass.ds(n, 1), :, :].rearrange("p o f k -> p (o f k)")
                W3 = VW * 3
                for t in range(NT):
                    o = acc[h % 2][:, t // 4, (t % 4) * W3:(t % 4 + 1) * W3]
                    od = o[:, W3 // 2:]
                    mm(o, emptyb[:, t * P:(t + 1) * P], csn, start=True, stop=False)
                    for c in range(NT):
                        mm(o, Hm[h % 2][:, c, t * P:(t + 1) * P], hi[:, c, :], start=False, stop=False)
                    for c in range(NT):
                        last = mm(od, GtN[:, c, t * P:(t + 1) * P], hi[:, c, W3 // 2:], start=False,
                                  stop=c == NT - 1)
                last.then_inc(hd_ps, 1)

            def transposes(b):
                pe.wait_ge(hc_ok, b + 1)
                for t in range(NT):
                    last = nc.tensor.transpose(XT[:, t * P:(t + 1) * P], hc[:, t, :], ident[:])
                last.then_inc(hT_ps, 1)

            def out_proj(b):
                pe.wait_ge(xres_ld, (b + 1) * 16)
                if not is_first(b):
                    pe.wait_ge(y_ok, b)
                y1 = [OPb[t // 4][:, (t % 4) * D:(t % 4 + 1) * D] for t in range(NT)]
                for k in range(2):
                    mm(OPb[k], ident[:], xres[:, 4 * k:4 * k + 4, :], start=True, stop=False)
                pe.wait_ge(hT_ok, b + 1)
                for t in range(NT):
                    last = mm(y1[t], hT[:, t * P:(t + 1) * P], WoT[:], start=False, stop=t % 4 == 3)
                last.then_inc(op_ps, 1)

            def l1_batch(b):
                for h in range(1, H):
                    if is_first(b) and h == 1:
                        pe.wait_ge(es_ok, BS - 1)
                    head(b, h)
                    if is_first(b):
                        if h == T_X1T:
                            transpose_x1(BS - 1, BS)
                        if h == T_PROJ:
                            pe.wait_ge(red_ok, T_PROJ)
                            proj(BS - 1)
                            transpose_es(BS - 1)
                            pe.wait_ge(es_ok, BS)
                    if not is_first(b):
                        if h == 1:
                            transposes(b - 1)
                        if h == 3:

                            out_proj(b - 1)
                if not is_last(b):
                    head(b + 1, 0)

            head(0, 0)
            l1_batch(0)
            with pe.Fori(1, BS - 1) as b:
                l1_batch(b)
            l1_batch(BS - 1)
            transposes(BS - 1)
            out_proj(BS - 1)


_INS = ['x', 'adj', 'L0_gnn_W', 'L0_gnn_a', 'L1_gnn_W', 'L1_gnn_a_src', 'L1_gnn_a_dst', 'L1_gnn_beta_tilde',
        'L1_gnn_W_out']


def kernel(**inputs):
    import numpy as _np
    import concourse.bacc as _bacc
    from concourse import mybir as _mybir
    from concourse.bass_utils import run_bass_kernel_spmd as _run

    nc = _bacc.Bacc("TRN2", target_bir_lowering=False, num_devices=1)
    arrays, args = {}, []
    for name in _INS:
        a = _np.ascontiguousarray(inputs[name])
        if a.ndim == 0:
            a = a.reshape(1)
        arrays[f"in_{name}_dram"] = a
        args.append(nc.dram_tensor(f"in_{name}_dram", a.shape, _mybir.dt.from_np(a.dtype), kind="ExternalInput").ap())
    out = nc.dram_tensor("out_0_dram", (BS, N, D), F32, kind="ExternalOutput").ap()
    gnn_kernel(nc, *args, out)
    r = _run(nc, [arrays], core_ids=[0])
    return r.results[0]["out_0_dram"]
```
